# Optimizing a Trainium2 kernel written in Bass

```python
import numpy as np
import jax
import jax.numpy as jnp

def _softmax(x, axis=-1):
    return jax.nn.softmax(x, axis=axis)

def _gelu(x):
    return jax.nn.gelu(x, approximate=True)

def _silu(x):
    return jax.nn.silu(x)

def _sigmoid(x):
    return jax.nn.sigmoid(x)

def _layernorm(x, axis=-1, eps=1e-05):
    m = jnp.mean(x, axis=axis, keepdims=True)
    v = jnp.var(x, axis=axis, keepdims=True)
    return (x - m) / jnp.sqrt(v + eps)

def _scatter_add(tgt, idx, src, axis=0):
    return tgt.at[idx].add(src)

def _segment_sum(src, seg, n):
    return jax.ops.segment_sum(src, seg, n)
kernel_name = 'mk_adj_seq_d2_adj_r2_edc3fb'

def setup_inputs(seed: int=0):
    np.random.seed(seed)
    _w = jnp.asarray

    def _rec_inputs():
        import jax
        import jax.numpy as jnp
        _gk = jax.random.key(seed)
        x = -0.0002928 + 1 * jax.random.normal(jax.random.fold_in(_gk, 1), (64, 128, 256), jnp.float32)
        _a = jax.random.bernoulli(jax.random.fold_in(_gk, 2), 0.015625, (64, 128, 128))
        _a = jnp.logical_or(_a, jnp.swapaxes(_a, -1, -2))
        _a = jnp.logical_or(_a, jnp.eye(128, dtype=bool))
        _af = _a.astype(jnp.float32)
        adj = _af
        return (x, adj)
    x, adj = _rec_inputs()

    def _L0_gnn_setup():
        import jax, jax.numpy as jnp
        import numpy as np
        import math
        D_MODEL = 256
        NHEAD = 8
        HEAD_DIM = D_MODEL // NHEAD
        LN_EPS = 1e-05

        def _layernorm(x, g, b):
            mu = jnp.mean(x, axis=-1, keepdims=True)
            var = jnp.mean(jnp.square(x - mu), axis=-1, keepdims=True)
            return (x - mu) * jax.lax.rsqrt(var + LN_EPS) * g + b
        key = jax.random.key(seed)
        ks = jax.random.split(key, 12)
        B, N, D = (4, 1024, D_MODEL)
        s = 1.0 / math.sqrt(D)
        inp = {'hidden': jax.random.normal(ks[0], (B, N, D), jnp.float32), 'adjacency': (jax.random.uniform(ks[1], (B, N, N)) > 0.98).astype(jnp.float32), 'Wq': jax.random.normal(ks[2], (D, D), jnp.float32) * s, 'bq': jnp.zeros((D,), jnp.float32), 'Wk': jax.random.normal(ks[3], (D, D), jnp.float32) * s, 'bk': jnp.zeros((D,), jnp.float32), 'Wv': jax.random.normal(ks[4], (D, D), jnp.float32) * s, 'bv': jnp.zeros((D,), jnp.float32), 'Wo': jax.random.normal(ks[5], (D, D), jnp.float32) * s, 'bo': jnp.zeros((D,), jnp.float32), 'g1': jnp.ones((D,), jnp.float32), 'b1': jnp.zeros((D,), jnp.float32), 'g2': jnp.ones((D,), jnp.float32), 'b2': jnp.zeros((D,), jnp.float32), 'Wf1': jax.random.normal(ks[6], (D, 4 * D), jnp.float32) * s, 'bf1': jnp.zeros((4 * D,), jnp.float32), 'Wf2': jax.random.normal(ks[7], (4 * D, D), jnp.float32) * (1.0 / math.sqrt(4 * D)), 'bf2': jnp.zeros((D,), jnp.float32)}
        return inp
    _L0_gnn_all = _L0_gnn_setup()
    _L0_gnn_in = {k: v for k, v in _L0_gnn_all.items() if k in ('Wq', 'bq', 'Wk', 'bk', 'Wv', 'bv', 'Wo', 'bo', 'g1', 'b1', 'g2', 'b2', 'Wf1', 'bf1', 'Wf2', 'bf2')}
    del _L0_gnn_all

    def _L1_gnn_setup():
        import jax, jax.numpy as jnp
        import numpy as np
        EPS = 1e-06
        ALPHA = 0.2

        def layer_norm(x, g, b):
            mu = jnp.mean(x, axis=-1, keepdims=True)
            var = jnp.mean(jnp.square(x - mu), axis=-1, keepdims=True)
            return (x - mu) * jax.lax.rsqrt(var + EPS) * g + b

        def graph_attention(x, bias, W, a_src, a_dst):
            B, N, D = x.shape
            H, Dh = a_src.shape
            h = jnp.einsum('bnd,dhk->bhnk', x, W.reshape(D, H, Dh))
            s = jnp.einsum('bhnk,hk->bhn', h, a_src)
            t = jnp.einsum('bhnk,hk->bhn', h, a_dst)
            e = jax.nn.leaky_relu(s[:, :, :, None] + t[:, :, None, :], ALPHA)
            e = e + bias[:, None, :, :]
            attn = jax.nn.softmax(e, axis=-1)
            out = jnp.einsum('bhij,bhjk->bhik', attn, h)
            return out.transpose(0, 2, 1, 3).reshape(B, N, H * Dh)
        key = jax.random.key(seed)
        ks = jax.random.split(key, 8)
        B, N, D, H = (2, 1024, 256, 8)
        Dh = D // H
        sc = 1.0 / np.sqrt(D)
        return {'x': jax.random.normal(ks[0], (B, N, D), jnp.float32), 'bias': jax.random.normal(ks[1], (B, N, N), jnp.float32), 'W1': jax.random.normal(ks[2], (D, D), jnp.float32) * sc, 'a_src1': jax.random.normal(ks[3], (H, Dh), jnp.float32) * sc, 'a_dst1': jax.random.normal(ks[4], (H, Dh), jnp.float32) * sc, 'g1': jnp.ones((D,), jnp.float32), 'b1': jnp.zeros((D,), jnp.float32), 'W2': jax.random.normal(ks[5], (D, D), jnp.float32) * sc, 'a_src2': jax.random.normal(ks[6], (1, D), jnp.float32) * sc, 'a_dst2': jax.random.normal(ks[7], (1, D), jnp.float32) * sc, 'g2': jnp.ones((D,), jnp.float32), 'b2': jnp.zeros((D,), jnp.float32)}
    _L1_gnn_all = _L1_gnn_setup()
    _L1_gnn_in = {k: v for k, v in _L1_gnn_all.items() if k in ('W1', 'a_src1', 'a_dst1', 'g1', 'b1', 'W2', 'a_src2', 'a_dst2', 'g2', 'b2')}
    del _L1_gnn_all
    return {'x': x, 'adj': adj, 'L0_gnn_Wq': _L0_gnn_in['Wq'], 'L0_gnn_bq': _L0_gnn_in['bq'], 'L0_gnn_Wk': _L0_gnn_in['Wk'], 'L0_gnn_bk': _L0_gnn_in['bk'], 'L0_gnn_Wv': _L0_gnn_in['Wv'], 'L0_gnn_bv': _L0_gnn_in['bv'], 'L0_gnn_Wo': _L0_gnn_in['Wo'], 'L0_gnn_bo': _L0_gnn_in['bo'], 'L0_gnn_g1': _L0_gnn_in['g1'], 'L0_gnn_b1': _L0_gnn_in['b1'], 'L0_gnn_g2': _L0_gnn_in['g2'], 'L0_gnn_b2': _L0_gnn_in['b2'], 'L0_gnn_Wf1': _L0_gnn_in['Wf1'], 'L0_gnn_bf1': _L0_gnn_in['bf1'], 'L0_gnn_Wf2': _L0_gnn_in['Wf2'], 'L0_gnn_bf2': _L0_gnn_in['bf2'], 'L1_gnn_W1': _L1_gnn_in['W1'], 'L1_gnn_a_src1': _L1_gnn_in['a_src1'], 'L1_gnn_a_dst1': _L1_gnn_in['a_dst1'], 'L1_gnn_g1': _L1_gnn_in['g1'], 'L1_gnn_b1': _L1_gnn_in['b1'], 'L1_gnn_W2': _L1_gnn_in['W2'], 'L1_gnn_a_src2': _L1_gnn_in['a_src2'], 'L1_gnn_a_dst2': _L1_gnn_in['a_dst2'], 'L1_gnn_g2': _L1_gnn_in['g2'], 'L1_gnn_b2': _L1_gnn_in['b2']}

def reference(x, adj, L0_gnn_Wq, L0_gnn_bq, L0_gnn_Wk, L0_gnn_bk, L0_gnn_Wv, L0_gnn_bv, L0_gnn_Wo, L0_gnn_bo, L0_gnn_g1, L0_gnn_b1, L0_gnn_g2, L0_gnn_b2, L0_gnn_Wf1, L0_gnn_bf1, L0_gnn_Wf2, L0_gnn_bf2, L1_gnn_W1, L1_gnn_a_src1, L1_gnn_a_dst1, L1_gnn_g1, L1_gnn_b1, L1_gnn_W2, L1_gnn_a_src2, L1_gnn_a_dst2, L1_gnn_g2, L1_gnn_b2):
    import jax
    import jax.numpy as jnp

    def _L0_gnn_ref(hidden, adjacency, Wq, bq, Wk, bk, Wv, bv, Wo, bo, g1, b1, g2, b2, Wf1, bf1, Wf2, bf2):
        import jax, jax.numpy as jnp
        import numpy as np
        import math
        D_MODEL = 256
        NHEAD = 8
        HEAD_DIM = D_MODEL // NHEAD
        LN_EPS = 1e-05

        def _layernorm(x, g, b):
            mu = jnp.mean(x, axis=-1, keepdims=True)
            var = jnp.mean(jnp.square(x - mu), axis=-1, keepdims=True)
            return (x - mu) * jax.lax.rsqrt(var + LN_EPS) * g + b
        B, N, D = hidden.shape
        H, Hd = (NHEAD, HEAD_DIM)
        normed = _layernorm(hidden, g1, b1)
        q = (normed @ Wq + bq).reshape(B, N, H, Hd).transpose(0, 2, 1, 3)
        k = (normed @ Wk + bk).reshape(B, N, H, Hd).transpose(0, 2, 1, 3)
        v = (normed @ Wv + bv).reshape(B, N, H, Hd).transpose(0, 2, 1, 3)
        logits = jnp.einsum('bhnd,bhmd->bhnm', q, k) / math.sqrt(Hd)
        adj = adjacency[:, None, :, :]
        logits = logits + (2.0 * adj - 1.0)
        weights = jax.nn.softmax(logits, axis=-1)
        weights = weights * (0.25 + 0.75 * adj)
        weights = weights / jnp.maximum(weights.sum(axis=-1, keepdims=True), 1e-06)
        attended = jnp.einsum('bhnm,bhmd->bhnd', weights, v)
        attended = attended.transpose(0, 2, 1, 3).reshape(B, N, D)
        hidden = hidden + attended @ Wo + bo
        h2 = _layernorm(hidden, g2, b2)
        ff = jax.nn.gelu(h2 @ Wf1 + bf1, approximate=False) @ Wf2 + bf2
        return hidden + ff

    def _L1_gnn_ref(x, bias, W1, a_src1, a_dst1, g1, b1, W2, a_src2, a_dst2, g2, b2):
        import jax, jax.numpy as jnp
        import numpy as np
        EPS = 1e-06
        ALPHA = 0.2

        def layer_norm(x, g, b):
            mu = jnp.mean(x, axis=-1, keepdims=True)
            var = jnp.mean(jnp.square(x - mu), axis=-1, keepdims=True)
            return (x - mu) * jax.lax.rsqrt(var + EPS) * g + b

        def graph_attention(x, bias, W, a_src, a_dst):
            B, N, D = x.shape
            H, Dh = a_src.shape
            h = jnp.einsum('bnd,dhk->bhnk', x, W.reshape(D, H, Dh))
            s = jnp.einsum('bhnk,hk->bhn', h, a_src)
            t = jnp.einsum('bhnk,hk->bhn', h, a_dst)
            e = jax.nn.leaky_relu(s[:, :, :, None] + t[:, :, None, :], ALPHA)
            e = e + bias[:, None, :, :]
            attn = jax.nn.softmax(e, axis=-1)
            out = jnp.einsum('bhij,bhjk->bhik', attn, h)
            return out.transpose(0, 2, 1, 3).reshape(B, N, H * Dh)
        attn_in = layer_norm(x, g1, b1)
        attn = graph_attention(attn_in, bias, W1, a_src1, a_dst1) + x
        attn_in2 = layer_norm(attn, g2, b2)
        out = graph_attention(attn_in2, bias, W2, a_src2, a_dst2) + attn
        return out
    x = _L0_gnn_ref(x, adj, L0_gnn_Wq, L0_gnn_bq, L0_gnn_Wk, L0_gnn_bk, L0_gnn_Wv, L0_gnn_bv, L0_gnn_Wo, L0_gnn_bo, L0_gnn_g1, L0_gnn_b1, L0_gnn_g2, L0_gnn_b2, L0_gnn_Wf1, L0_gnn_bf1, L0_gnn_Wf2, L0_gnn_bf2)
    x = _L1_gnn_ref(x, adj, L1_gnn_W1, L1_gnn_a_src1, L1_gnn_a_dst1, L1_gnn_g1, L1_gnn_b1, L1_gnn_W2, L1_gnn_a_src2, L1_gnn_a_dst2, L1_gnn_g2, L1_gnn_b2)
    return x

_drawn_inputs = setup_inputs


def setup_inputs(seed=0):
    import zlib

    import numpy as np

    out = dict(_drawn_inputs(seed))
    spreads = {'L0_gnn_bq': (0.0, 0.304),
     'L0_gnn_bk': (0.0, 0.8),
     'L0_gnn_bv': (0.0, 0.1),
     'L0_gnn_bo': (0.0, 0.1),
     'L0_gnn_g1': (1.0, 0.2),
     'L0_gnn_b1': (0.0, 0.1),
     'L0_gnn_g2': (1.0, 0.2),
     'L0_gnn_b2': (0.0, 0.1),
     'L0_gnn_bf1': (0.0, 0.1),
     'L0_gnn_bf2': (0.0, 0.1),
     'L1_gnn_g1': (1.0, 0.2),
     'L1_gnn_b1': (0.0, 0.1),
     'L1_gnn_g2': (1.0, 0.2),
     'L1_gnn_b2': (0.0, 0.1)}
    factors = {'L1_gnn_a_src1': 5.222, 'L1_gnn_a_src2': 3.045}
    for name, (base, spread) in spreads.items():
        noise = np.random.default_rng([zlib.crc32(name.encode()), seed]).standard_normal(out[name].shape)
        drawn = base * np.exp(spread * noise) if base else spread * noise
        out[name] = jnp.asarray(drawn.astype(out[name].dtype))
    for name, factor in factors.items():
        out[name] = (out[name] * factor).astype(out[name].dtype)
    return out
```

```python
from contextlib import ExitStack

import concourse.bass as bass
from concourse import mybir

F32 = mybir.dt.float32
F32R = mybir.dt.float32r
ALU = mybir.AluOpType
ACT = mybir.ActivationFunctionType
AX = mybir.AxisListType.X

P = 128
D = 256
KT = D // P
G = 4
W4 = G * P
H = 8
HD = D // H
HA = HD + 1
FF = 4 * D
FT = FF // P
LOGIT_SCALE = HD ** -0.5
LOG_3_4 = -0.2876820724517809
EXP_LIMIT = 66.0
ROWS = 40
TROW = 96


def wait_for(eng, sem, value):
    if isinstance(value, int) and value <= 0:
        return
    eng.wait_ge(sem, value)


def build(nc, x, adj, wq, bq, wk, bk, wv, bv, wo, bo, g1, b1, g2, b2, wf1, bf1, wf2, bf2,
          w1, as1, ad1, lg1, lb1, w2, as2, ad2, lg2, lb2, out):
    NG = x.shape[0]
    NC = NG // G
    assert x.shape[1:] == (P, D) and NC >= 4 and NC % 2 == 0

    ctx = ExitStack()
    with ctx:
        def sb(name, shape, dt=F32):
            return ctx.enter_context(nc.sbuf_tensor(name, shape, dt))

        def sem(name):
            return ctx.enter_context(nc.semaphore(name))

        def psum(name):
            return ctx.enter_context(nc.psum_tensor(name, [P, 512], F32))

        x_all = sb("x_all", [P, NG * D])
        adj_in = [sb(f"adj_in{r}", [P, G, P]) for r in range(2)]
        ident = sb("ident", [P, P])
        neg_half = sb("neg_half", [P, G])
        eps_l0 = sb("eps_l0", [P, G])
        eps_l1 = sb("eps_l1", [P, G])
        whl = {}
        for name, kt, n in (("wq", KT, D), ("wk", KT, D), ("wv", KT, D), ("wo", KT, D), ("wf1", KT, FF),
                            ("wf2", FT, D), ("w1", KT, D), ("w2", KT, D), ("wst1", KT, P), ("wst2", KT, P)):
            whl[name] = [sb(f"{name}_{part}", [P, kt, n], F32R) for part in ("hi", "lo")]
        ones33 = sb("ones33", [33, P], F32R)
        row_bias = {n: sb(f"row_{n}", [33, D], F32R) for n in ("bo", "bf2", "c1", "c2")}
        cols = sb("cols", [P, 40])
        bcol = sb("bcol", [P, 14])
        sel = sb("sel", [ROWS, H, P], F32R)
        sgn = sb("sgn", [ROWS, 1])
        scl = sb("scl", [ROWS, 1])
        cb = [sb(f"cb{n}", [ROWS, 1]) for n in range(2)]
        exp_bias = sb("exp_bias", [P, 1])
        st = sb("st", [P, G, 6])
        mv = sb("mv", [P, G, 2])
        ve = sb("ve", [P, G])
        rstd = sb("rstd", [P, G])
        xn = sb("xn", [P, G, D])
        xh = sb("xh", [P, KT, W4], F32R)
        xl = sb("xl", [P, KT, W4], F32R)

        REGION = 52 * 1024
        base_of_region = (nc.sbuf_base + 31) // 32 * 32
        sb("region", [P, REGION // 4 + 8])

        def overlay():
            at = [base_of_region]

            def alloc(name, shape, dt=F32):
                t = nc.alloc_sbuf_tensor_at(name, shape, dt, offset=at[0])
                n = 4
                for d in shape[1:]:
                    n *= d
                at[0] += (n + 31) // 32 * 32
                assert at[0] - base_of_region <= REGION, name
                return t
            return alloc

        o = overlay()
        stage = {"wq": o("s_wq", [P, KT, D]), "wk": o("s_wk", [P, KT, D]), "wv": o("s_wv", [P, KT, D]),
                 "wo": o("s_wo", [P, KT, D]), "wf1": o("s_wf1", [P, KT, FF]), "wf2": o("s_wf2", [P, FT, D]),
                 "w1": o("s_w1", [P, KT, D]), "w2": o("s_w2", [P, KT, D])}
        a_bc = [o(f"a_bc{n}", [P, D]) for n in range(4)]
        rows_in = o("rows_in", [1, 2, D])
        prod = o("prod", [P, KT, D])
        wa = o("wa", [P, 2, 2, KT, H])
        wag = o("wag", [P, 2, 2, KT, H])
        wst = o("wst", [P, 2, KT, P])
        wc = o("wc", [P, 2, KT, ROWS])
        grp = o("grp", [ROWS, 16])
        bo_row = o("bo_row", [1, D])
        bv_col = o("bv_col", [P, KT])

        o = overlay()
        q_sb = [o(f"q{r}", [P, 2, W4]) for r in range(2)]
        k_sb = [o(f"k{r}", [P, 2, W4]) for r in range(2)]
        kd_sb = [o(f"kd{r}", [P, 2, 4, P]) for r in range(2)]
        v_sb = [o(f"v{r}", [P, G, H * HA]) for r in range(2)]
        ft_sb = [o(f"ft{r}", [P, G, P]) for r in range(2)]
        e_sb = o("e_sb", [P, H, P])
        pt_sb = o("pt_sb", [P, H, P])
        att = o("att", [P, D])
        ah = o("ah", [P, D], F32R)
        al = o("al", [P, D], F32R)
        mx = o("mx", [P, H])
        nmx = o("nmx", [P, H])
        rsum = o("rsum", [P, H])
        rinv = o("rinv", [P, H])

        o = overlay()
        gh = o("gh", [P, FT, W4], F32R)
        gl = o("gl", [P, FT, W4], F32R)
        gf = [o(f"gf{r}", [P, W4]) for r in range(2)]

        o = overlay()
        gt_sb = [o(f"gt{r}", [P, G, P]) for r in range(2)]
        hb = [o(f"hb{r}", [P, G * H * HA]) for r in range(2)]
        bq_sb = [o(f"bqs{r}", [P, G, 24]) for r in range(2)]
        rp = [o(f"rp{r}", [ROWS, W4], F32R) for r in range(2)]
        tmx = o("tmx", [24, G])
        tms = o("tms", [ROWS, G])
        u_sb = o("u_sb", [ROWS, W4])
        rb = o("rb", [P, W4])
        pp = [o(f"pp{r}", [P, G, P]) for r in range(2)]
        atc = [o(f"atc{r}", [P, D]) for r in range(2)]
        crec = o("crec", [P, G, H])
        y_sb = [o(f"y{r}", [P, G, D]) for r in range(2)]

        F = [psum("F0"), psum("F1")]
        BK = ctx.enter_context(nc.psum_tensor("BK", [P, 6, 512], F32))
        L_ps = BK[:, 0:2, :].rearrange("p a (h n) -> p (a h) n", n=P)
        ET_ps = BK[:, 2:4, :].rearrange("p a (h n) -> p (a h) n", n=P)
        O_ps = BK[:, 4, 0:H * HA].rearrange("p (h c) -> p h c", c=HA)
        WO_ps = BK[:, 5, 0:D]

        w_in = [sem("w_in_qkvo"), sem("w_in_ff"), sem("w_in_l1"), sem("w_in_small")]
        s_ident = sem("s_ident")
        setup_dve = sem("setup_dve")
        setup_pe = sem("setup_pe")
        x_in = [sem("x_in0"), sem("x_in1")]
        adj_ld = [sem("adj_ld0"), sem("adj_ld1")]
        ln_st, ln_mv, ln_ve, ln_rs, ln_xn, ln_t, ln_xh, ln_xl = (
            sem(n) for n in ("ln_st", "ln_mv", "ln_ve", "ln_rs", "ln_xn", "ln_t", "ln_xh", "ln_xl"))
        adj_t = sem("adj_t")
        sp_gates = sem("sp_gates")
        kd_ld = [sem("kd_ld0"), sem("kd_ld1")]
        a_et, a_ft, a_qk, a_qkev, a_v, a_vev = (sem(n) for n in ("a_et", "a_ft", "a_qk", "a_qkev", "a_v", "a_vev"))
        a_l, a_mx, a_nm, a_e, a_tt, a_pt, a_o, a_rs, a_ri, a_att, a_at, a_ah, a_al, a_wo, a_x = (
            sem(n) for n in ("a_l", "a_mx", "a_nm", "a_e", "a_tt", "a_pt", "a_o", "a_rs", "a_ri", "a_att",
                             "a_at", "a_ah", "a_al", "a_wo", "a_x"))
        b_h, b_gh, b_gl, b_o, b_x = (sem(n) for n in ("b_h", "b_gh", "b_gl", "b_o", "b_x"))
        c_gt, c_st, c_rows, c_rb, c_bqt, c_bq, c_h, c_hb, c_one, c_zero = (
            sem(n) for n in ("c_gt", "c_st", "c_rows", "c_rb", "c_bqt", "c_bq", "c_h", "c_hb", "c_one", "c_zero"))
        c_bc, c_pp, c_o, c_rec, c_att, c_x = (sem(n) for n in ("c_bc", "c_pp", "c_o", "c_rec", "c_att", "c_x"))
        d_bc, d_pp, d_o, d_rec, d_y = (sem(n) for n in ("d_bc", "d_pp", "d_o", "d_rec", "d_y"))
        y_out = [sem("y_out0"), sem("y_out1")]

        CA, CB, CC, CD = 0, NC, 2 * NC, 3 * NC
        EPS = {CA: eps_l0, CB: eps_l0, CC: eps_l1, CD: eps_l1}

        def xs(i, g):
            return x_all[:, bass.ds((i * G + g) * D, D)]

        def chunks(eng, step, n=NC):
            for i in range(2):
                step(i, 0, i)
            with eng.Fori(1, n // 2 - 1) as t:
                step(t * 2, t, 0)
                step(t * 2 + 1, t, 1)
            for i in range(n - 2, n):
                step(i, n // 2 - 1, i % 2)

        setup_at = {}
        block = ctx.enter_context(nc.Block())

        small_cols = [(b1, 0), (bq, 2), (bk, 4), (bv, 6), (g1, 8), (g2, 10), (b2, 12), (bf1, 14),
                      (lb1, 22), (lg1, 24), (lb2, 26), (lg2, 28)]

        @block.vector
        def _(dve):
            def stats(c, i, g):
                dve.bn_stats(st[:, g, :], xs(i, g)).then_inc(ln_st, 1)

            def aggr(c):
                for g in range(G):
                    dve.bn_aggr(mv[:, g, :], st[:, g, :]).then_inc(ln_mv, 1)

            def normalise(c, i):
                dve.wait_ge(ln_rs, c + 1)
                wait_for(dve, ln_t, c * KT)
                for g in range(G):
                    dve.tensor_scalar(xn[:, g, :], xs(i, g), mv[:, g, 0:1], rstd[:, g:g + 1],
                                      ALU.subtract, ALU.mult).then_inc(ln_xn, 1)

            def ln_lo(c):
                for kt in range(KT):
                    dve.wait_ge(ln_xh, c * KT + kt + 1)
                    dve.tensor_tensor(xl[:, kt, :], F[kt][:], xh[:, kt, :].bitcast(F32), ALU.subtract).then_inc(ln_xl, 1)

            steps = [0]

            def done(ins):
                steps[0] += 1
                ins.then_inc(setup_dve, 1)

            def settle():
                dve.wait_ge(setup_dve, steps[0])

            def split(name, gain_at):
                hi, lo, w = whl[name][0], whl[name][1], stage[name]
                kts = w.shape[1]
                for kt in range(kts):
                    if gain_at is None:
                        done(dve.tensor_copy(hi[:, kt, :], w[:, kt, :]))
                    else:
                        done(dve.tensor_scalar(hi[:, kt, :], w[:, kt, :], cols[:, gain_at + kt:gain_at + kt + 1], None, ALU.mult))
                settle()
                for kt in range(kts):
                    if gain_at is None:
                        done(dve.tensor_tensor(lo[:, kt, :], w[:, kt, :], hi[:, kt, :].bitcast(F32), ALU.subtract))
                    else:
                        done(dve.scalar_tensor_tensor(out=lo[:, kt, :], in0=w[:, kt, :], scalar=cols[:, gain_at + kt:gain_at + kt + 1],
                                                      in1=hi[:, kt, :].bitcast(F32), op0=ALU.mult, op1=ALU.subtract))

            dve.wait_ge(x_in[0], 16)
            for g in range(G):
                stats(0, 0, g)
            dve.wait_ge(ln_st, G)
            aggr(0)
            for n in range(2):
                done(dve.memset(wst[:, n], 0.0))
                done(dve.memset(wc[:, n], 0.0))
                done(dve.memset(wa[:, n], 0.0))
            for r in row_bias.values():
                done(dve.memset(r[:].bitcast(F32), 0.0))
            done(dve.memset(ones33[:].bitcast(F32), 1.0))
            done(dve.memset(exp_bias[:], LOG_3_4 - 1.0))
            dve.wait_ge(w_in[3], 16 * (len(small_cols) + 6))
            dve.wait_ge(w_in[0], 64)
            split("wq", 8)
            split("wk", 8)
            split("wv", 8)
            split("wo", None)
            normalise(0, 0)
            dve.wait_ge(w_in[1], 32)
            split("wf1", 10)
            split("wf2", None)
            dve.wait_ge(w_in[2], 32)
            split("w1", 24)
            split("w2", 28)
            dve.wait_ge(s_ident, 5)
            done(dve.tensor_reduce(grp[:], ident[0:ROWS, :].rearrange("p (a b) -> p a b", b=8), AX, ALU.add))
            done(dve.tensor_tensor(sel[:], ident[0:ROWS, 0:H].unsqueeze(2).to_broadcast([ROWS, H, P]),
                                   ident[0:ROWS, 32:32 + H].unsqueeze(2).to_broadcast([ROWS, H, P]), ALU.add))
            settle()
            done(dve.tensor_tensor(grp[:, 8:9], grp[:, 0:1], grp[:, 4:5], ALU.add))
            done(dve.tensor_tensor(grp[:, 9:10], grp[:, 1:2], grp[:, 2:3], ALU.add))
            settle()
            done(dve.tensor_tensor(sgn[:], grp[:, 8:9], grp[:, 9:10], ALU.subtract))
            done(dve.tensor_tensor(grp[:, 10:11], grp[:, 8:9], grp[:, 2:3], ALU.subtract))
            settle()
            done(dve.scalar_tensor_tensor(out=scl[:], in0=grp[:, 10:11], scalar=0.8, in1=grp[:, 1:2], op0=ALU.mult, op1=ALU.add))
            for layer, (name, heads, gain_at) in enumerate((("w1", H, 24), ("w2", 1, 28))):
                w = stage[name]
                for side in range(2):
                    settle()
                    done(dve.tensor_tensor(prod[:], w[:], a_bc[2 * layer + side][:].unsqueeze(1).to_broadcast([P, KT, D]), ALU.mult))
                    settle()
                    done(dve.tensor_reduce(wa[:, layer, side, :, 0:heads], prod[:].rearrange("p k (h d) -> p k h d", h=heads), AX, ALU.add))
                settle()
                for side in range(2):
                    done(dve.tensor_tensor(wag[:, layer, side], wa[:, layer, side],
                                           cols[:, gain_at:gain_at + KT].unsqueeze(2).to_broadcast([P, KT, H]), ALU.mult))
                settle()
                for at, side in ((0, 0), (8, 1), (16, 1), (32, 0), (TROW, 1), (TROW + 8, 1), (TROW + 16, 1)):
                    done(dve.tensor_copy(wst[:, layer, :, at:at + H], wag[:, layer, side]))
                for at in (0, 32):
                    done(dve.tensor_tensor(wc[:, layer, :, at:at + H], wa[:, layer, 0], wa[:, layer, 1], ALU.add))
                settle()
                hi, lo = whl[f"wst{layer + 1}"]
                done(dve.tensor_copy(hi[:], wst[:, layer]))
                settle()
                done(dve.tensor_tensor(lo[:], wst[:, layer], hi[:].bitcast(F32), ALU.subtract))
            setup_at["weights"] = steps[0]
            dve.wait_ge(setup_pe, 1)
            done(dve.tensor_tensor(bcol[:, 0:4], F[0][:, 0:4], cols[:, 2:6], ALU.add))
            done(dve.tensor_tensor(bcol[:, 6:14], F[0][:, 6:14], cols[:, 14:22], ALU.add))
            done(dve.tensor_tensor(bv_col[:], F[0][:, 4:6], cols[:, 6:8], ALU.add))
            for n in range(2):
                done(dve.tensor_copy(cb[n][:], F[0][0:ROWS, 14 + n:15 + n]))
            setup_at["columns"] = steps[0]
            dve.wait_ge(setup_pe, 2)
            done(dve.tensor_tensor(bo_row[:], BK[0:1, 0, 0:D], rows_in[:, 0, :], ALU.add))
            settle()
            for name, src in (("bo", bo_row[:]), ("bf2", rows_in[:, 1, :]), ("c1", BK[0:1, 1, 0:D]), ("c2", BK[0:1, 2, 0:D])):
                done(dve.tensor_copy(row_bias[name][0:1, :], src))
                settle()
                done(dve.tensor_tensor(row_bias[name][32:33, :], src, row_bias[name][0:1, :].bitcast(F32), ALU.subtract))
            settle()
            for r in range(2):
                done(dve.memset(v_sb[r][:], 1.0))
                done(dve.memset(kd_sb[r][:], 0.0))
            setup_at["all"] = steps[0]

            def a_ft_out(i, par):
                dve.wait_ge(a_et, i + 1)
                f = ft_sb[par][:].rearrange("p g n -> p (g n)")
                dve.scalar_tensor_tensor(out=f, in0=F[0][:], scalar=1.0 / 3.0, in1=f, op0=ALU.add, op1=ALU.mult).then_inc(a_ft, 1)

            def a_max(s):
                dve.wait_ge(a_l, s + 1)
                dve.tensor_reduce(mx[:], L_ps, AX, ALU.max).then_inc(a_mx, 1)
                dve.wait_ge(a_mx, s + 1)
                wait_for(dve, a_e, s)
                dve.tensor_scalar(nmx[:], mx[:], -LOGIT_SCALE, None, ALU.mult).then_inc(a_nm, 1)

            def a_norm(s):
                dve.wait_ge(a_o, s + 1)
                dve.tensor_scalar(rsum[:], O_ps[:, :, HD], 1e-6, None, ALU.max).then_inc(a_rs, 1)
                dve.wait_ge(a_rs, s + 1)
                dve.reciprocal(rinv[:], rsum[:]).then_inc(a_ri, 1)
                dve.wait_ge(a_ri, s + 1)
                wait_for(dve, a_at, s)
                dve.tensor_tensor(att[:].rearrange("p (h d) -> p h d", d=HD), O_ps[:, :, 0:HD],
                                  rinv[:].unsqueeze(2).to_broadcast([P, H, HD]), ALU.mult).then_inc(a_att, 1)

            def a_al_out(s):
                dve.wait_ge(a_ah, s + 1)
                dve.tensor_tensor(al[:], WO_ps, ah[:].bitcast(F32), ALU.subtract).then_inc(a_al, 1)

            def a_pt_out(s, par, g):
                dve.wait_ge(a_tt, s + 1)
                wait_for(dve, a_o, s)
                dve.tensor_tensor(pt_sb[:], ET_ps, ft_sb[par][:, g, :].unsqueeze(1).to_broadcast([P, H, P]), ALU.mult).then_inc(a_pt, 1)

            def a_resid(i, g, s):
                dve.wait_ge(a_wo, s + 1)
                dve.tensor_tensor(xs(i, g), WO_ps, xs(i, g), ALU.add).then_inc(a_x, 1)

            def a_ln(i, g, half, par):
                final = isinstance(i, int) and i == NC - 1
                nxt = 0 if final else i + 1
                if g == 1:
                    if final:
                        dve.wait_ge(a_x, G)
                    elif par == 0:
                        dve.wait_ge(x_in[1], (half + 1) * 16)
                    else:
                        dve.wait_ge(x_in[0], (half + 2) * 16)
                    stats(i + CA + 1, nxt, 0)
                    stats(i + CA + 1, nxt, 1)
                if g == 2:
                    stats(i + CA + 1, nxt, 2)
                    stats(i + CA + 1, nxt, 3)
                    dve.wait_ge(ln_st, (i + CA + 2) * G)
                if g == 3:
                    normalise(i + CA + 1, nxt)

            def a_step(i, half, par):
                first = isinstance(i, int) and i == 0
                for g in range(G):
                    s = i * G + (g - G)
                    if not first:
                        a_max(s)
                    prev = not (first or (isinstance(s, int) and s == 0))
                    if prev:
                        a_norm(s - 1)
                    if g == 0:
                        ln_lo(i + CA)
                    if prev:
                        a_al_out(s - 1)
                    if g == 0:
                        a_ft_out(i, par)
                    a_ln(i, g, half, par)
                    if not first:
                        a_pt_out(s, 1 - par, g)
                    if g == 2:
                        aggr(i + CA + 1)
                    if prev:
                        a_resid(*((i - 2, G - 1) if g == 0 else (i - 1, g - 1)), s - 1)
            chunks(dve, a_step)
            for g in range(G):
                s = (NC - 1) * G + g
                a_max(s)
                a_norm(s - 1)
                a_al_out(s - 1)
                a_pt_out(s, (NC - 1) % 2, g)
                a_resid((s - 1) // G, (s - 1) % G, s - 1)
            a_norm(NG - 1)
            a_al_out(NG - 1)
            a_resid(NC - 1, G - 1, NG - 1)

            def b_step(i, half, par):
                final = isinstance(i, int) and i == NC - 1
                nxt = 0 if final else i + 1
                for f in range(FT):
                    if f == G:
                        dve.wait_ge(ln_st, (i + CB + 2) * G)
                    dve.wait_ge(b_gh, i * FT + f + 1)
                    dve.tensor_tensor(gl[:, f, :], gf[f % 2][:], gh[:, f, :].bitcast(F32), ALU.subtract).then_inc(b_gl, 1)
                    if f == 0:
                        dve.wait_ge(*((b_x, G) if final else (a_x, (i + 2) * G)))
                    if f < G:
                        stats(i + CB + 1, nxt, f)
                    if f == G:
                        aggr(i + CB + 1)
                    if f == FT - 2:
                        normalise(i + CB + 1, nxt)
                if not final:
                    ln_lo(i + CB + 1)
                for g in range(G):
                    dve.wait_ge(b_o, i * G + g + 1)
                    dve.tensor_tensor(xs(i, g), BK[:, 4 + g % 2, 0:D], xs(i, g), ALU.add).then_inc(b_x, 1)
            ln_lo(CB)
            chunks(dve, b_step)

            def rows_max(e):
                dve.wait_ge(c_st, e + 1)
                dve.tensor_reduce(tmx[:], F[1][TROW:TROW + 24, :].rearrange("p (g n) -> p g n", n=P), AX, ALU.max).then_inc(c_rows, 1)
                dve.wait_ge(c_rows, e * 7 + 1)
                dve.tensor_scalar(tms[0:24, :], tmx[:], sgn[0:24, 0:1], None, ALU.mult).then_inc(c_rows, 1)
                dve.tensor_copy(tms[32:40, :], tmx[0:8, :]).then_inc(c_rows, 1)

            def rows_exponent(e, layer):
                dve.wait_ge(c_rows, e * 7 + 3)
                dve.scalar_tensor_tensor(out=u_sb[:].rearrange("p (g n) -> p g n", n=P),
                                         in0=F[1][0:ROWS, :].rearrange("p (g n) -> p g n", n=P), scalar=cb[layer][:, 0:1],
                                         in1=tms[:].unsqueeze(2).to_broadcast([ROWS, G, P]), op0=ALU.add, op1=ALU.add).then_inc(c_rows, 1)
                dve.wait_ge(c_rows, e * 7 + 4)
                dve.tensor_scalar(u_sb[:], u_sb[:], scl[:, 0:1], EXP_LIMIT, ALU.mult, ALU.min).then_inc(c_rows, 1)

            def rows_split(e, par):
                dve.wait_ge(c_rb, e + 1)
                dve.tensor_copy(rp[par][:], rb[0:ROWS, :]).then_inc(c_rows, 1)
                dve.wait_ge(c_rows, e * 7 + 6)
                dve.tensor_tensor(rp[par][32:40, :], rb[32:40, :], rp[par][32:40, :].bitcast(F32), ALU.subtract).then_inc(c_rows, 1)

            def hb_view(par, layer):
                if layer == 0:
                    return hb[par][:].rearrange("p (g h c) -> p g h c", g=G, h=H)
                return hb[par][:, 0:G * (D + 1)].rearrange("p (g h c) -> p g h c", g=G, h=1)

            def bq_out(e, par, layer):
                heads = (H, 1)[layer]
                dve.wait_ge(c_bqt, e + 1)
                dve.tensor_copy(bq_sb[par][:], F[1][:].rearrange("p (g c) -> p g c", c=P)[:, :, 0:24]).then_inc(c_bq, 1)
                dve.wait_ge(c_bq, e + 1)
                dve.tensor_copy(hb_view(par, layer)[:, :, :, D // heads], bq_sb[par][:, :, 8:8 + heads]).then_inc(c_one, 1)

            def hb_out(e, par, layer, n):
                heads = (H, 1)[layer]
                dve.wait_ge(c_h, e * 2 + n + 1)
                for g in range(2 * n, 2 * n + 2):
                    r = dve.tensor_tensor(hb_view(par, layer)[:, g, :, 0:D // heads],
                                          F[n][:, (g % 2) * D:(g % 2 + 1) * D].rearrange("p (h d) -> p h d", h=heads),
                                          bq_sb[par][:, g, 8:8 + heads].unsqueeze(2).to_broadcast([P, heads, D // heads]), ALU.mult)
                r.then_inc(c_hb, 1)

            def c_front(i, par, first, piece):
                c, e, layer = i + first, i + (first - CC), (first - CC) // NC
                final = isinstance(i, int) and i == NC - 1
                nxt = 0 if final else i + 1
                more = not (final and first == CD)
                if piece == 0:
                    ln_lo(c)
                if piece == 1 and more:
                    if first == CC:
                        dve.wait_ge(*((c_x, G) if final else (b_x, (i + 2) * G)))
                    else:
                        dve.wait_ge(c_x, (i + 2) * G)
                    stats(c + 1, nxt, 0)
                    stats(c + 1, nxt, 1)
                if piece == 2 and more:
                    stats(c + 1, nxt, 2)
                    stats(c + 1, nxt, 3)
                if piece == 3:
                    rows_max(e)
                if piece == 4:
                    rows_exponent(e, layer)
                if piece == 5:
                    if more:
                        dve.wait_ge(ln_st, (c + 2) * G)
                    rows_split(e, par)
                    if more:
                        aggr(c + 1)
                if piece == 6:
                    bq_out(e, par, layer)
                    hb_out(e, par, layer, 0)
                if piece == 7:
                    if more:
                        normalise(c + 1, nxt)
                    hb_out(e, par, layer, 1)

            def c_scale(i, par, h):
                dve.wait_ge(c_bc, i * H + h + 1)
                dve.wait_ge(c_gt, i + 1)
                wait_for(dve, c_o, i * H + (h - 1))
                for g in range(G):
                    r = dve.scalar_tensor_tensor(out=pp[h % 2][:, g, :], in0=BK[:, h % 2, g * P:(g + 1) * P],
                                                 scalar=bq_sb[par][:, g, 16 + h:17 + h], in1=gt_sb[par][:, g, :],
                                                 op0=ALU.max, op1=ALU.mult)
                r.then_inc(c_pp, 1)

            def c_norm(i):
                for g in range(G):
                    o_ps = BK[:, 2 + g, 0:H * HA].rearrange("p (h c) -> p h c", c=HA)
                    dve.wait_ge(c_o, (i + 1) * H)
                    dve.reciprocal(crec[:, g, :], o_ps[:, :, HD]).then_inc(c_rec, 1)
                for g in range(G):
                    o_ps = BK[:, 2 + g, 0:H * HA].rearrange("p (h c) -> p h c", c=HA)
                    dve.wait_ge(c_rec, i * G + g + 1)
                    wait_for(dve, c_x, i * G + (g - 1))
                    dve.tensor_tensor(atc[g % 2][:].rearrange("p (h d) -> p h d", d=HD), o_ps[:, :, 0:HD],
                                      crec[:, g, :].unsqueeze(2).to_broadcast([P, H, HD]), ALU.mult).then_inc(c_att, 1)

            def c1_step(i, half, par):
                back = not (isinstance(i, int) and i == 0)
                for h in range(H):
                    if back:
                        c_scale(i - 1, 1 - par, h)
                    c_front(i, par, CC, h)
                if back:
                    c_norm(i - 1)
            dve.wait_ge(b_x, NG)
            dve.memset(tms[:], 0.0).then_inc(c_zero, 1)
            dve.memset(rb[:], 0.0).then_inc(c_zero, 1)
            dve.wait_ge(c_zero, 2)
            chunks(dve, c1_step)
            for h in range(H):
                c_scale(NC - 1, (NC - 1) % 2, h)
            c_norm(NC - 1)

            def d_scale(i, par):
                dve.wait_ge(d_bc, i + 1)
                dve.wait_ge(c_gt, i + NC + 1)
                wait_for(dve, d_o, i * G)
                for g in range(G):
                    dve.scalar_tensor_tensor(out=pp[0][:, g, :], in0=BK[:, 0, g * P:(g + 1) * P],
                                             scalar=bq_sb[par][:, g, 16:17], in1=gt_sb[par][:, g, :],
                                             op0=ALU.max, op1=ALU.mult).then_inc(d_pp, 1)

            def d_norm(i, half, par):
                for g in range(G):
                    dve.wait_ge(d_o, i * G + g + 1)
                    dve.reciprocal(crec[:, g, 0:1], BK[:, 2 + g, D:D + 1]).then_inc(d_rec, 1)
                wait_for(dve, y_out[par], half * 16)
                for g in range(G):
                    dve.wait_ge(d_rec, i * G + g + 1)
                    dve.scalar_tensor_tensor(out=y_sb[par][:, g, :], in0=BK[:, 2 + g, 0:D], scalar=crec[:, g, 0:1],
                                             in1=xs(i, g), op0=ALU.mult, op1=ALU.add).then_inc(d_y, 1)

            def c2_step(i, half, par):
                back = not (isinstance(i, int) and i == 0)
                if back:
                    d_scale(i - 1, 1 - par)
                for piece in range(4):
                    c_front(i, par, CD, piece)
                if back:
                    d_norm(i - 1, half - (1 - par), 1 - par)
                for piece in range(4, 8):
                    c_front(i, par, CD, piece)
            chunks(dve, c2_step)
            d_scale(NC - 1, 1)
            d_norm(NC - 1, NC // 2 - 1, 1)

        @block.sync
        def _(sp):
            def gate(sem, value):
                if isinstance(value, int) and value <= 0:
                    return
                sp.wait_ge(sem, value)
                sp.sem_inc(sp_gates, 1)

            def kp(w):
                return w.rearrange("(k p) n -> p k n", p=P)

            for w, name in ((wq, "wq"), (wk, "wk"), (wv, "wv"), (wo, "wo")):
                sp.dma_start(stage[name][:], kp(w)).then_inc(w_in[0], 16)

            def load_adj(i, half, par):
                sp.dma_start(adj_in[par][:], adj[bass.ds(i * G, G)].rearrange("g p n -> p g n")).then_inc(adj_ld[par], 16)

            def load_a(i, half, par):
                gate(x_in[par], half * 16)
                sp.dma_start(x_all[:, bass.ds(i * G * D, G * D)].rearrange("p (g d) -> p g d", d=D),
                             x[bass.ds(i * G, G)].rearrange("g p d -> p g d")).then_inc(x_in[par], 16)
                gate(adj_t, i - 1)
                load_adj(i, half, par)
                if isinstance(i, int) and i == 0:
                    for w, name in ((wf1, "wf1"), (wf2, "wf2")):
                        sp.dma_start(stage[name][:], kp(w)).then_inc(w_in[1], 16)
                    for w, name in ((w1, "w1"), (w2, "w2")):
                        sp.dma_start(stage[name][:], kp(w)).then_inc(w_in[2], 16)

            def spread_k(i, par):
                gate(a_qkev, i * 4 + 4)
                for g in range(G):
                    gate(a_l, i * G + (g - 1))
                    for r in range(4):
                        rows = slice(HD * r, HD * r + HD)
                        sp.dma_start(kd_sb[g % 2][rows, :, r, :], k_sb[par][rows, :, g * P:(g + 1) * P]).then_inc(kd_ld[g % 2], 16)

            def a_step(i, half, par):
                if not (isinstance(i, int) and i == NC - 1):
                    load_a(i + 1, half + par, 1 - par)
                if not (isinstance(i, int) and i == 0):
                    spread_k(i - 1, 1 - par)
            load_a(0, 0, 0)
            sp.wait_ge(setup_dve, setup_at["all"])
            chunks(sp, a_step)
            spread_k(NC - 1, (NC - 1) % 2)

            for first in (CC, CD):
                def load_c(i, half, par, first=first):
                    gate(adj_t, i + (first - CB - 1))
                    load_adj(i, half, par)
                    if first == CD:
                        store(i, half, par)

                def store(i, half, par):
                    if isinstance(i, int) and i == 0:
                        return
                    gate(d_y, i * G)
                    sp.dma_start(out[bass.ds(i * G - G, G)].rearrange("g p d -> p g d"), y_sb[1 - par][:]).then_inc(y_out[1 - par], 16)
                chunks(sp, load_c)
            gate(d_y, NC * G)
            sp.dma_start(out[(NC - 1) * G:NC * G].rearrange("g p d -> p g d"), y_sb[1][:]).then_inc(y_out[1], 16)
            sp.wait_ge(y_out[0], 16 * (NC // 2))
            sp.wait_ge(y_out[1], 16 * (NC // 2))

        @block.gpsimd
        def _(pool):
            pool.memset(ident[:], 0.0).then_inc(s_ident, 1)
            pool.memset(neg_half[:], -0.5).then_inc(s_ident, 1)
            pool.memset(eps_l0[:], 1e-5).then_inc(s_ident, 1)
            pool.memset(eps_l1[:], 1e-6).then_inc(s_ident, 1)
            pool.wait_ge(s_ident, 4)
            pool.affine_select(out=ident[:], in_=ident[:], compare_op=ALU.not_equal, fill=1.0, base=0,
                               pattern=[[-1, P]], channel_multiplier=1).then_inc(s_ident, 1)

            def rstd_of(c, eps):
                pool.wait_ge(ln_mv, c * G + G)
                pool.tensor_tensor(ve[:], mv[:, :, 1], eps[:], ALU.add).then_inc(ln_ve, 1)
                pool.wait_ge(ln_ve, c + 1)
                pool.tensor_tensor(rstd[:], ve[:], neg_half[:], ALU.pow).then_inc(ln_rs, 1)

            rstd_of(0, EPS[CA])
            for first, last in ((CA, NC - 1), (CB, NC - 1), (CC, NC - 1), (CD, NC - 1)):
                def norms(i, half, par, first=first):
                    final = isinstance(i, int) and i == NC - 1
                    if not (final and first == CD):
                        rstd_of(i + first + 1, EPS[first + NC] if final else EPS[first])
                    if first == CC and not (isinstance(i, int) and i == 0):
                        residual(i - 1)

                def residual(i):
                    for g in range(G):
                        pool.wait_ge(c_att, i * G + g + 1)
                        pool.tensor_tensor(xs(i, g), atc[g % 2][:], xs(i, g), ALU.add).then_inc(c_x, 1)
                chunks(pool, norms)
                if first == CC:
                    residual(NC - 1)

        @block.scalar
        def _(act):
            for vec, at in small_cols:
                n = vec.shape[0] // P
                with nc.allow_non_contiguous_dma("a vector as columns"):
                    act.dma_start(cols[:, at:at + n], vec.rearrange("(k p) -> p k", p=P)).then_inc(w_in[3], 16)
            for n, a in enumerate((as1, ad1, as2, ad2)):
                act.dma_start(a_bc[n][:], a.rearrange("h k -> (h k)").partition_broadcast(P)).then_inc(w_in[3], 16)
            for n, r in enumerate((bo, bf2)):
                act.dma_start(rows_in[:, n, :], r.rearrange("(a d) -> a d", a=1)).then_inc(w_in[3], 16)

            def ln_hi(c):
                for kt in range(KT):
                    act.wait_ge(ln_t, c * KT + kt + 1)
                    act.activation(xh[:, kt, :], F[kt][:], ACT.Copy).then_inc(ln_xh, 1)

            def a_adj(i, par):
                act.wait_ge(adj_t, i + 1)
                act.activation(ft_sb[par][:].rearrange("p g n -> p (g n)"), F[0][:], ACT.Exp,
                               bias=exp_bias[:, 0:1], scale=2.0).then_inc(a_et, 1)

            def a_qk_out(i, par, n):
                dst = (q_sb, k_sb)[n // 2][par][:, n % 2, :]
                act.wait_ge(a_qk, i * 4 + n + 1)
                act.activation(dst, F[(n + 1) % 2][:], ACT.Identity, bias=bcol[:, n:n + 1]).then_inc(a_qkev, 1)

            def a_v_out(i, par, n):
                act.wait_ge(a_v, i * 2 + n + 1)
                for e in range(2):
                    r = act.activation(v_sb[par][:, 2 * n + e, :].rearrange("p (h c) -> p h c", c=HA)[:, :, 0:HD],
                                       F[1 - n][:, e * D:(e + 1) * D].rearrange("p (h c) -> p h c", c=HD), ACT.Copy)
                r.then_inc(a_vev, 1)

            def a_front(i, par, g):
                if g == 0:
                    a_adj(i, par)
                    a_qk_out(i, par, 0)
                if g == 1:
                    a_qk_out(i, par, 2)
                if g == 2:
                    a_v_out(i, par, 0)

            def a_front_early(i, par, g):
                if g == 0:
                    ln_hi(i + CA)
                if g == 1:
                    a_qk_out(i, par, 1)
                if g == 2:
                    a_qk_out(i, par, 3)
                if g == 3:
                    a_v_out(i, par, 1)

            def a_exps(s):
                act.wait_ge(a_nm, s + 1)
                wait_for(act, a_tt, s)
                for h in range(H):
                    r = act.activation(e_sb[:, h, :], L_ps[:, h, :], ACT.Exp, bias=nmx[:, h:h + 1], scale=LOGIT_SCALE)
                r.then_inc(a_e, 1)

            def a_ah_out(s):
                act.wait_ge(a_at, s + 1)
                act.activation(ah[:], WO_ps, ACT.Copy).then_inc(a_ah, 1)

            def a_step(i, half, par):
                for g in range(G):
                    s = i * G + (g - G)
                    first = isinstance(i, int) and i == 0
                    if g == 0:
                        a_front_early(i, par, g)
                    if not first:
                        a_exps(s)
                    if g > 0:
                        a_front_early(i, par, g)
                    if not (first or (isinstance(s, int) and s == 0)):
                        a_ah_out(s - 1)
                    a_front(i, par, g)
            act.wait_ge(setup_dve, setup_at["all"])
            chunks(act, a_step)
            for g in range(G):
                s = (NC - 1) * G + g
                a_exps(s)
                a_ah_out(s - 1)
            a_ah_out(NG - 1)

            def b_step(i, half, par):
                for f in range(FT):
                    act.wait_ge(b_h, i * FT + f + 1)
                    if f == 0:
                        wait_for(act, b_o, i * G)
                    wait_for(act, b_gl, i * FT + (f - 1))
                    act.activation(gf[f % 2][:], BK[:, f % 4, :], ACT.Gelu, bias=bcol[:, 6 + f:7 + f])
                    act.activation(gh[:, f, :], BK[:, f % 4, :], ACT.Gelu, bias=bcol[:, 6 + f:7 + f]).then_inc(b_gh, 1)
                if not (isinstance(i, int) and i == NC - 1):
                    ln_hi(i + CB + 1)
            ln_hi(CB)
            act.wait_ge(a_x, NG)
            chunks(act, b_step)

            for first in (CC, CD):
                def c_step(i, half, par, first=first):
                    c = i + first
                    ln_hi(c)
                    act.wait_ge(adj_t, c - NC + 1)
                    act.activation(gt_sb[par][:].rearrange("p g n -> p (g n)"), F[0][:], ACT.Exp).then_inc(c_gt, 1)
                    act.wait_ge(c_rows, (c - CC) * 7 + 5)
                    act.activation(rb[0:ROWS, :], u_sb[:], ACT.Exp).then_inc(c_rb, 1)
                if first == CC:
                    act.wait_ge(c_zero, 2)
                chunks(act, c_step)

        @block.tensor
        def _(pe):
            def three(dst, w_hi, w_lo, m_hi, m_lo, start, stop):
                pe.matmul(dst, w_hi, m_hi, start=start, stop=False)
                pe.matmul(dst, w_hi, m_lo, start=False, stop=False)
                return pe.matmul(dst, w_lo, m_hi, start=False, stop=stop)

            def wide(dst, name, at):
                hi, lo = whl[name]
                for kt in range(KT):
                    r = three(dst, hi[:, kt, at:at + P], lo[:, kt, at:at + P], xh[:, kt, :], xl[:, kt, :], kt == 0, kt == KT - 1)
                return r

            def tall(dst, name, g, bias, start):
                hi, lo = whl[name]
                if bias is not None:
                    pe.matmul(dst, ones33[:], row_bias[bias][:], start=start, stop=False, skip_group_check=True)
                for kt in range(KT):
                    n = slice(g * P, (g + 1) * P)
                    pe.matmul(dst, xh[:, kt, n], hi[:, kt, :], start=start and bias is None and kt == 0, stop=False, skip_group_check=True)
                    pe.matmul(dst, xl[:, kt, n], hi[:, kt, :], start=False, stop=False, skip_group_check=True)
                    r = pe.matmul(dst, xh[:, kt, n], lo[:, kt, :], start=False, stop=(kt == KT - 1), skip_group_check=True)
                return r

            def ln_turn(c):
                pe.wait_ge(ln_xn, c * G + G)
                for kt in range(KT):
                    for g in range(G):
                        r = pe.transpose(F[kt][:, g * P:(g + 1) * P], xn[:, g, kt * P:(kt + 1) * P], ident[:])
                    r.then_inc(ln_t, 1)

            pe.wait_ge(setup_dve, setup_at["weights"])
            pe.wait_ge(s_ident, 5)
            col = 0
            for name, b_at, tiles in (("wq", 0, 2), ("wk", 0, 2), ("wv", 0, 2), ("wf1", 12, FT)):
                for m in range(tiles):
                    for kt in range(KT):
                        pe.matmul(F[0][:, col:col + 1], stage[name][:, kt, m * P:(m + 1) * P], cols[:, b_at + kt:b_at + kt + 1],
                                  start=(kt == 0), stop=(kt == KT - 1), skip_group_check=True)
                    col += 1
            for layer, b_at in ((0, 22), (1, 26)):
                for kt in range(KT):
                    r = pe.matmul(F[0][0:ROWS, col:col + 1], wc[:, layer, kt, :], cols[:, b_at + kt:b_at + kt + 1],
                                  start=(kt == 0), stop=(kt == KT - 1), skip_group_check=True)
                col += 1
            r.then_inc(setup_pe, 1)
            pe.wait_ge(setup_dve, setup_at["columns"])
            for bank, name, vec, at in ((0, "wo", bv_col, 0), (1, "w1", cols, 22), (2, "w2", cols, 26)):
                for kt in range(KT):
                    r = pe.matmul(BK[0:1, bank, 0:D], vec[:, at + kt:at + kt + 1], stage[name][:, kt, :],
                                  start=(kt == 0), stop=(kt == KT - 1))
            r.then_inc(setup_pe, 1)
            pe.wait_ge(setup_dve, setup_at["all"])

            def a_proj(i, n):
                wait_for(pe, *(((ln_xl, (i + CA) * KT + 2)), (a_ft, i + 1), (a_qkev, i * 4 + 1), (a_qkev, i * 4 + 2))[n])
                wide(F[(n + 1) % 2][:], ("wq", "wk")[n // 2], (n % 2) * P).then_inc(a_qk, 1)

            def a_vproj(i, n):
                pe.wait_ge(a_qkev, i * 4 + 3 + n)
                for e in range(2):
                    r = tall(F[1 - n][:, e * D:(e + 1) * D], "wv", 2 * n + e, None, e == 0)
                r.then_inc(a_v, 1)

            def adj_turn(c, half, par, first):
                before = {CA: 0, CC: NC // 2, CD: NC}[first]
                pe.wait_ge(adj_ld[par], (half + 1 + before) * 16)
                pe.wait_ge(ln_xl, c * KT + 1)
                for g in range(G):
                    r = pe.transpose(F[0][:, g * P:(g + 1) * P], adj_in[par][:, g, :], ident[:])
                r.then_inc(adj_t, 1)

            def a_front_a(i, half, par, g):
                if g == 0:
                    wait_for(pe, a_vev, i * 2)
                    ln_turn(i + CA)
                if g == 1:
                    a_proj(i, 1)
                if g == 2:
                    a_proj(i, 3)
                if g == 3:
                    a_vproj(i, 1)

            def a_front_b(i, half, par, g):
                if g == 0:
                    adj_turn(i + CA, half, par, CA)
                    a_proj(i, 0)
                if g == 1:
                    a_proj(i, 2)
                if g == 2:
                    a_vproj(i, 0)

            def a_logits(s, i, par, g):
                pe.wait_ge(a_qkev, i * 4 + 4)
                wait_for(pe, a_e, s)
                pe.wait_ge(kd_ld[g % 2], (i * 2 + (g // 2 + 1)) * 64)
                for t in range(2):
                    r = pe.matmul(BK[:, t, :], q_sb[par][:, t, g * P:(g + 1) * P], kd_sb[g % 2][:, t].rearrange("p h n -> p (h n)"),
                                  start=True, stop=True)
                r.then_inc(a_l, 1)

            def a_turn(s):
                pe.wait_ge(a_e, s + 1)
                wait_for(pe, a_pt, s)
                for h in range(H):
                    r = pe.transpose(ET_ps[:, h, :], e_sb[:, h, :], ident[:])
                r.then_inc(a_tt, 1)

            def a_av(s, i, par, g):
                pe.wait_ge(a_vev, i * 2 + 2)
                pe.wait_ge(a_pt, s + 1)
                wait_for(pe, a_att, s)
                for h in range(H):
                    r = pe.matmul(O_ps[:, h, :], pt_sb[:, h, :], v_sb[par][:, g, h * HA:(h + 1) * HA], start=True, stop=True)
                r.then_inc(a_o, 1)

            def a_attn_turn(s):
                pe.wait_ge(a_att, s + 1)
                wait_for(pe, a_x, s)
                for kt in range(KT):
                    r = pe.transpose(BK[:, 5, kt * P:(kt + 1) * P], att[:, kt * P:(kt + 1) * P], ident[:])
                r.then_inc(a_at, 1)

            def a_out(s):
                pe.wait_ge(a_al, s + 1)
                hi, lo = whl["wo"]
                pe.matmul(WO_ps, ones33[:], row_bias["bo"][:], start=True, stop=False)
                for kt in range(KT):
                    n = slice(kt * P, (kt + 1) * P)
                    pe.matmul(WO_ps, ah[:, n], hi[:, kt, :], start=False, stop=False)
                    pe.matmul(WO_ps, al[:, n], hi[:, kt, :], start=False, stop=False)
                    r = pe.matmul(WO_ps, ah[:, n], lo[:, kt, :], start=False, stop=(kt == KT - 1))
                r.then_inc(a_wo, 1)

            def a_step(i, half, par):
                first = isinstance(i, int) and i == 0
                for g in range(G):
                    s = i * G + (g - G)
                    prev = not (first or (isinstance(s, int) and s == 0))
                    if not first:
                        a_logits(s, i - 1, 1 - par, g)
                    if prev:
                        a_av(s - 1, *((i - 2, par, G - 1) if g == 0 else (i - 1, 1 - par, g - 1)))
                    a_front_a(i, half, par, g)
                    if prev:
                        a_attn_turn(s - 1)
                    a_front_b(i, half, par, g)
                    if not first:
                        a_turn(s)
                    if prev:
                        a_out(s - 1)
            chunks(pe, a_step)
            for g in range(G):
                s = (NC - 1) * G + g
                a_logits(s, NC - 1, (NC - 1) % 2, g)
                a_av(s - 1, (s - 1) // G, (s - 1) // G % 2, (s - 1) % G)
                a_attn_turn(s - 1)
                a_turn(s)
                a_out(s - 1)
            a_av(NG - 1, NC - 1, (NC - 1) % 2, G - 1)
            a_attn_turn(NG - 1)
            a_out(NG - 1)

            def b_step(i, half, par):
                pe.wait_ge(ln_xl, (i + CB) * KT + 2)
                for f in range(FT):
                    wait_for(pe, b_gh, i * FT + (f - 3))
                    wide(BK[:, f % 4, :], "wf1", f * P).then_inc(b_h, 1)
                if not (isinstance(i, int) and i == NC - 1):
                    ln_turn(i + CB + 1)
                hi, lo = whl["wf2"]
                for g in range(G):
                    dst = BK[:, 4 + g % 2, 0:D]
                    n = slice(g * P, (g + 1) * P)
                    wait_for(pe, b_x, i * G + (g - 1))
                    pe.matmul(dst, ones33[:], row_bias["bf2"][:], start=True, stop=False)
                    for f in range(FT):
                        pe.wait_ge(b_gl, i * FT + f + 1)
                        pe.matmul(dst, gh[:, f, n], hi[:, f, :], start=False, stop=False)
                        pe.matmul(dst, gl[:, f, n], hi[:, f, :], start=False, stop=False)
                        r = pe.matmul(dst, gh[:, f, n], lo[:, f, :], start=False, stop=(f == FT - 1))
                    r.then_inc(b_o, 1)
            pe.wait_ge(a_vev, 2 * NC)
            ln_turn(CB)
            pe.wait_ge(a_x, NG)
            chunks(pe, b_step)

            def c_front(i, half, par, first, piece):
                c, e, layer = i + first, i + (first - CC), (first - CC) // NC
                if piece == 0:
                    wait_for(pe, c_hb, e * 2)
                    if isinstance(c, int) and c == CC:
                        pe.wait_ge(ln_xl, c * KT)
                    ln_turn(c)
                if piece == 1:
                    adj_turn(c, half, par, first)
                if piece == 2:
                    pe.wait_ge(ln_xl, c * KT + 2)
                    wide(F[1][:], ("wst1", "wst2")[layer], 0).then_inc(c_st, 1)
                if piece == 3:
                    pe.wait_ge(c_gt, e + 1)
                    for g in range(2):
                        r = tall(F[0][:, g * D:(g + 1) * D], ("w1", "w2")[layer], g, ("c1", "c2")[layer], g == 0)
                    r.then_inc(c_h, 1)
                if piece == 5:
                    pe.wait_ge(c_rb, e + 1)
                    for g in range(G):
                        r = pe.transpose(F[1][:, g * P:(g + 1) * P], rb[:, g * P:(g + 1) * P], ident[:])
                    r.then_inc(c_bqt, 1)
                if piece == 7:
                    pe.wait_ge(c_bq, e + 1)
                    for g in range(2, 4):
                        r = tall(F[1][:, (g - 2) * D:(g - 1) * D], ("w1", "w2")[layer], g, ("c1", "c2")[layer], g == 2)
                    r.then_inc(c_h, 1)

            def c_bcast(i, par, h):
                pe.wait_ge(c_rows, i * 7 + 7)
                wait_for(pe, c_pp, i * H + (h - 1))
                pe.matmul(BK[:, h % 2, :], sel[:, h, :], rp[par][:], start=True, stop=True).then_inc(c_bc, 1)

            def c_av(i, par, h):
                pe.wait_ge(c_pp, i * H + h + 1)
                if h == 0:
                    pe.wait_ge(c_hb, i * 2 + 2)
                    pe.wait_ge(c_one, i + 1)
                    wait_for(pe, c_att, i * G)
                for g in range(G):
                    r = pe.matmul(BK[:, 2 + g, h * HA:(h + 1) * HA], pp[h % 2][:, g, :],
                                  hb[par][:, (g * H + h) * HA:(g * H + h + 1) * HA], start=True, stop=True)
                r.then_inc(c_o, 1)

            def c1_step(i, half, par):
                back = not (isinstance(i, int) and i == 0)
                if back:
                    c_bcast(i - 1, 1 - par, 0)
                for h in range(H):
                    if back and h < H - 1:
                        c_bcast(i - 1, 1 - par, h + 1)
                    c_front(i, half, par, CC, h)
                    if back:
                        c_av(i - 1, 1 - par, h)
            pe.wait_ge(b_x, NG)
            chunks(pe, c1_step)
            last = (NC - 1) % 2
            c_bcast(NC - 1, last, 0)
            for h in range(H):
                if h < H - 1:
                    c_bcast(NC - 1, last, h + 1)
                c_av(NC - 1, last, h)

            def d_bcast(i, par):
                pe.wait_ge(c_rows, (i + NC) * 7 + 7)
                wait_for(pe, d_pp, i * G)
                pe.matmul(BK[:, 0, :], sel[:, 0, :], rp[par][:], start=True, stop=True).then_inc(d_bc, 1)

            def d_av(i, par):
                pe.wait_ge(c_hb, (i + NC) * 2 + 2)
                pe.wait_ge(c_one, i + NC + 1)
                for g in range(G):
                    pe.wait_ge(d_pp, i * G + g + 1)
                    wait_for(pe, d_y, i * G + (g - G + 1))
                    pe.matmul(BK[:, 2 + g, 0:D + 1], pp[0][:, g, :], hb[par][:, g * (D + 1):(g + 1) * (D + 1)],
                              start=True, stop=True).then_inc(d_o, 1)

            def c2_step(i, half, par):
                back = not (isinstance(i, int) and i == 0)
                if back:
                    d_bcast(i - 1, 1 - par)
                for piece in range(3):
                    c_front(i, half, par, CD, piece)
                if back:
                    d_av(i - 1, 1 - par)
                for piece in range(3, 8):
                    c_front(i, half, par, CD, piece)
            pe.wait_ge(c_att, NG)
            chunks(pe, c2_step)
            d_bcast(NC - 1, last)
            d_av(NC - 1, last)




_INS = ['x', 'adj', 'L0_gnn_Wq', 'L0_gnn_bq', 'L0_gnn_Wk', 'L0_gnn_bk', 'L0_gnn_Wv', 'L0_gnn_bv', 'L0_gnn_Wo', 'L0_gnn_bo',
        'L0_gnn_g1', 'L0_gnn_b1', 'L0_gnn_g2', 'L0_gnn_b2', 'L0_gnn_Wf1', 'L0_gnn_bf1', 'L0_gnn_Wf2', 'L0_gnn_bf2',
        'L1_gnn_W1', 'L1_gnn_a_src1', 'L1_gnn_a_dst1', 'L1_gnn_g1', 'L1_gnn_b1',
        'L1_gnn_W2', 'L1_gnn_a_src2', 'L1_gnn_a_dst2', 'L1_gnn_g2', 'L1_gnn_b2']


def kernel(**inputs):
    import numpy as _np
    import concourse.bacc as _bacc
    from concourse import mybir as _mybir
    from concourse.bass_utils import run_bass_kernel_spmd as _run

    nc = _bacc.Bacc("TRN2", target_bir_lowering=False, num_devices=1)
    arrays, args = {}, []
    for name in _INS:
        a = _np.ascontiguousarray(inputs[name])
        arrays[f"in_{name}_dram"] = a
        args.append(nc.dram_tensor(f"in_{name}_dram", a.shape, _mybir.dt.from_np(a.dtype), kind="ExternalInput").ap())
    args.append(nc.dram_tensor("out_0_dram", inputs["x"].shape, _mybir.dt.float32, kind="ExternalOutput").ap())
    build(nc, *args)
    r = _run(nc, [arrays], core_ids=[0])
    return r.results[0]["out_0_dram"]
```

```python
from contextlib import ExitStack

import concourse.bass as bass
from concourse import mybir

F32 = mybir.dt.float32
F32R = mybir.dt.float32r
ALU = mybir.AluOpType
ACT = mybir.ActivationFunctionType
AX = mybir.AxisListType.X

P = 128
D = 256
KT = D // P
G = 4
W4 = G * P
H = 8
HD = D // H
HA = HD + 1
FF = 4 * D
FT = FF // P
LOGIT_SCALE = HD ** -0.5
LOG_3_4 = -0.2876820724517809
EXP_LIMIT = 66.0
AVW = 96
ROWS = 40
TROW = 96


def wait_for(eng, sem, value):
    if isinstance(value, int) and value <= 0:
        return
    eng.wait_ge(sem, value)


def build(nc, x, adj, wq, bq, wk, bk, wv, bv, wo, bo, g1, b1, g2, b2, wf1, bf1, wf2, bf2,
          w1, as1, ad1, lg1, lb1, w2, as2, ad2, lg2, lb2, out):
    NG = x.shape[0]
    NC = NG // G
    assert x.shape[1:] == (P, D) and NC >= 4 and NC % 2 == 0

    ctx = ExitStack()
    with ctx:
        def sb(name, shape, dt=F32):
            return ctx.enter_context(nc.sbuf_tensor(name, shape, dt))

        def sem(name):
            return ctx.enter_context(nc.semaphore(name))

        def psum(name):
            return ctx.enter_context(nc.psum_tensor(name, [P, 512], F32))

        x_all = sb("x_all", [P, NG * D])
        adj_in = [sb(f"adj_in{r}", [P, G, P]) for r in range(2)]
        ident = sb("ident", [P, P])
        neg_half = sb("neg_half", [P, G])
        zero_g = sb("zero_g", [P, G])
        eps_l0 = sb("eps_l0", [P, G])
        eps_l1 = sb("eps_l1", [P, G])
        whl = {}
        for name, kt, n in (("wq", KT, D), ("wk", KT, D), ("wv", KT, D), ("wo", KT, D), ("wf1", KT, FF),
                            ("wf2", FT, D), ("w1", KT, D), ("w2", KT, D), ("wst1", KT, P), ("wst2", KT, P)):
            whl[name] = [sb(f"{name}_{part}", [P, kt, n], F32R) for part in ("hi", "lo")]
        ones33 = sb("ones33", [33, P], F32R)
        row_bias = {n: sb(f"row_{n}", [33, D], F32R) for n in ("bo", "bf2", "c1", "c2")}
        cols = sb("cols", [P, 40])
        bcol = sb("bcol", [P, 14])
        sel = sb("sel", [ROWS, H, P], F32R)
        sgn = sb("sgn", [ROWS, 1])
        scl = sb("scl", [ROWS, 1])
        cb = [sb(f"cb{n}", [ROWS, 1]) for n in range(2)]
        exp_bias = sb("exp_bias", [P, 1])
        st = sb("st", [P, G, 6])
        mv = sb("mv", [P, G, 2])
        ve = sb("ve", [P, G])
        rstd = sb("rstd", [P, G])
        neg_mr = sb("neg_mr", [P, G])
        xn = sb("xn", [P, G, D])
        xh = sb("xh", [P, KT, W4], F32R)
        xl = sb("xl", [P, KT, W4], F32R)

        REGION = 52 * 1024
        base_of_region = (nc.sbuf_base + 31) // 32 * 32
        sb("region", [P, REGION // 4 + 8])

        def overlay():
            at = [base_of_region]

            def alloc(name, shape, dt=F32):
                t = nc.alloc_sbuf_tensor_at(name, shape, dt, offset=at[0])
                n = 4
                for d in shape[1:]:
                    n *= d
                at[0] += (n + 31) // 32 * 32
                assert at[0] - base_of_region <= REGION, name
                return t
            return alloc

        o = overlay()
        stage = {"wq": o("s_wq", [P, KT, D]), "wk": o("s_wk", [P, KT, D]), "wv": o("s_wv", [P, KT, D]),
                 "wo": o("s_wo", [P, KT, D]), "wf1": o("s_wf1", [P, KT, FF]), "wf2": o("s_wf2", [P, FT, D]),
                 "w1": o("s_w1", [P, KT, D]), "w2": o("s_w2", [P, KT, D])}
        a_bc = [o(f"a_bc{n}", [P, D]) for n in range(4)]
        rows_in = o("rows_in", [1, 2, D])
        prod = o("prod", [P, KT, D])
        wa = o("wa", [P, 2, 2, KT, H])
        wag = o("wag", [P, 2, 2, KT, H])
        wst = o("wst", [P, 2, KT, P])
        wc = o("wc", [P, 2, KT, ROWS])
        grp = o("grp", [ROWS, 16])
        bo_row = o("bo_row", [1, D])
        bv_col = o("bv_col", [P, KT])

        o = overlay()
        q_sb = [o(f"q{r}", [P, 2, W4]) for r in range(2)]
        k_sb = [o(f"k{r}", [P, 2, W4]) for r in range(2)]
        kd_sb = [o(f"kd{r}", [P, 2, 4, P]) for r in range(2)]
        v_sb = [o(f"v{r}", [P, G * H * HA + AVW - HA]) for r in range(2)]
        ft_sb = [o(f"ft{r}", [P, G, P]) for r in range(2)]
        e_sb = o("e_sb", [P, H, P])
        pt_sb = o("pt_sb", [P, H, P])
        att = o("att", [P, D])
        ah = o("ah", [P, D], F32R)
        al = o("al", [P, D], F32R)
        mx = o("mx", [P, H])
        nmx = o("nmx", [P, H])
        rsum = o("rsum", [P, H])
        rinv = o("rinv", [P, H])

        o = overlay()
        gh = o("gh", [P, FT, W4], F32R)
        gl = o("gl", [P, FT, W4], F32R)
        gf = [o(f"gf{r}", [P, W4]) for r in range(2)]

        o = overlay()
        gt_sb = [o(f"gt{r}", [P, G, P]) for r in range(2)]
        hb = [o(f"hb{r}", [P, G * H * HA + AVW - HA]) for r in range(2)]
        bq_sb = [o(f"bqs{r}", [P, G, 24]) for r in range(2)]
        rp = [o(f"rp{r}", [ROWS, W4], F32R) for r in range(2)]
        tmx = o("tmx", [24, G])
        tms = o("tms", [ROWS, G])
        u_sb = o("u_sb", [ROWS, W4])
        rb = o("rb", [P, W4])
        pp = [o(f"pp{r}", [P, G, P]) for r in range(2)]
        o_sb = o("o_sb", [P, G, H * HA])
        atc = o("atc", [P, G, D])
        crec = o("crec", [P, G, H])
        y_sb = [o(f"y{r}", [P, G, D]) for r in range(2)]

        F = [psum("F0"), psum("F1")]
        BK = ctx.enter_context(nc.psum_tensor("BK", [P, 6, 512], F32))
        L_ps = BK[:, 0:2, :].rearrange("p a (h n) -> p (a h) n", n=P)
        ET_ps = BK[:, 2:4, :].rearrange("p a (h n) -> p (a h) n", n=P)
        O_ps = BK[:, 4, 0:H * HA].rearrange("p (h c) -> p h c", c=HA)

        D_O = (3, 4, 5, 3)

        def head_out(bank, h):
            return BK[:, bank, h * HA:h * HA + AVW]

        def head_in(t, g, h):
            return t[:, (g * H + h) * HA:(g * H + h) * HA + AVW]

        WO_ps = BK[:, 5, 0:D]

        w_in = [sem("w_in_qkvo"), sem("w_in_ff"), sem("w_in_l1"), sem("w_in_small")]
        s_ident = sem("s_ident")
        setup_dve = sem("setup_dve")
        setup_pe = sem("setup_pe")
        x_in = [sem("x_in0"), sem("x_in1")]
        adj_ld = [sem("adj_ld0"), sem("adj_ld1")]
        ln_st, ln_mv, ln_ve, ln_rs, ln_xn, ln_t, ln_xh, ln_xl = (
            sem(n) for n in ("ln_st", "ln_mv", "ln_ve", "ln_rs", "ln_xn", "ln_t", "ln_xh", "ln_xl"))
        ln_mr = sem("ln_mr")
        ln_nm = sem("ln_nm")
        adj_t = sem("adj_t")
        sp_gates = sem("sp_gates")
        kd_ld = [sem("kd_ld0"), sem("kd_ld1")]
        a_et, a_ft, a_qk, a_qkev, a_v, a_vev = (sem(n) for n in ("a_et", "a_ft", "a_qk", "a_qkev", "a_v", "a_vev"))
        a_l, a_mx, a_nm, a_e, a_tt, a_pt, a_o, a_rs, a_ri, a_att, a_at, a_ah, a_al, a_wo, a_x = (
            sem(n) for n in ("a_l", "a_mx", "a_nm", "a_e", "a_tt", "a_pt", "a_o", "a_rs", "a_ri", "a_att",
                             "a_at", "a_ah", "a_al", "a_wo", "a_x"))
        b_h, b_gh, b_gl, b_o, b_x = (sem(n) for n in ("b_h", "b_gh", "b_gl", "b_o", "b_x"))
        c_gt, c_st_done, c_rows, c_rb, c_bqt, c_bq, c_h, c_hb, c_one, c_zero = (
            sem(n) for n in ("c_gt", "c_st_done", "c_rows", "c_rb", "c_bqt", "c_bq", "c_h", "c_hb", "c_one", "c_zero"))
        c_rp, c_lo = sem("c_rp"), sem("c_lo")
        c_bc, c_pp, c_o, c_ev, c_rec, c_att, c_x = (sem(n) for n in ("c_bc", "c_pp", "c_o", "c_ev", "c_rec", "c_att", "c_x"))
        d_bc, d_pp, d_o, d_rec, d_y = (sem(n) for n in ("d_bc", "d_pp", "d_o", "d_rec", "d_y"))
        y_out = [sem("y_out0"), sem("y_out1")]

        CA, CB, CC, CD = 0, NC, 2 * NC, 3 * NC
        EPS = {CA: eps_l0, CB: eps_l0, CC: eps_l1, CD: eps_l1}

        def xs(i, g):
            return x_all[:, bass.ds((i * G + g) * D, D)]

        def chunks(eng, step, n=NC):
            for i in range(2):
                step(i, 0, i)
            with eng.Fori(1, n // 2 - 1) as t:
                step(t * 2, t, 0)
                step(t * 2 + 1, t, 1)
            for i in range(n - 2, n):
                step(i, n // 2 - 1, i % 2)

        setup_at = {}
        block = ctx.enter_context(nc.Block())

        small_cols = [(b1, 0), (bq, 2), (bk, 4), (bv, 6), (g1, 8), (g2, 10), (b2, 12), (bf1, 14),
                      (lb1, 22), (lg1, 24), (lb2, 26), (lg2, 28)]

        @block.vector
        def _(dve):
            def stats(c, i, g):
                dve.bn_stats(st[:, g, :], xs(i, g)).then_inc(ln_st, 1)

            def aggr(c):
                for g in range(G):
                    dve.bn_aggr(mv[:, g, :], st[:, g, :]).then_inc(ln_mv, 1)

            def normalise(c, i, graphs=range(G)):
                dve.wait_ge(ln_rs, c + 1)
                wait_for(dve, ln_t, c * KT)
                for g in graphs:
                    dve.tensor_scalar(xn[:, g, :], xs(i, g), mv[:, g, 0:1], rstd[:, g:g + 1],
                                      ALU.subtract, ALU.mult).then_inc(ln_xn, 1)

            def ln_lo(c):
                for kt in range(KT):
                    dve.wait_ge(ln_xh, c * KT + kt + 1)
                    dve.tensor_tensor(xl[:, kt, :], F[kt][:], xh[:, kt, :].bitcast(F32), ALU.subtract).then_inc(ln_xl, 1)

            steps = [0]

            def done(ins):
                steps[0] += 1
                ins.then_inc(setup_dve, 1)

            def settle():
                dve.wait_ge(setup_dve, steps[0])

            def split(name, gain_at):
                hi, lo, w = whl[name][0], whl[name][1], stage[name]
                kts = w.shape[1]
                for kt in range(kts):
                    if gain_at is None:
                        done(dve.tensor_copy(hi[:, kt, :], w[:, kt, :]))
                    else:
                        done(dve.tensor_scalar(hi[:, kt, :], w[:, kt, :], cols[:, gain_at + kt:gain_at + kt + 1], None, ALU.mult))
                settle()
                for kt in range(kts):
                    if gain_at is None:
                        done(dve.tensor_tensor(lo[:, kt, :], w[:, kt, :], hi[:, kt, :].bitcast(F32), ALU.subtract))
                    else:
                        done(dve.scalar_tensor_tensor(out=lo[:, kt, :], in0=w[:, kt, :], scalar=cols[:, gain_at + kt:gain_at + kt + 1],
                                                      in1=hi[:, kt, :].bitcast(F32), op0=ALU.mult, op1=ALU.subtract))

            dve.wait_ge(x_in[0], 16)
            for g in range(G):
                stats(0, 0, g)
            dve.wait_ge(ln_st, G)
            aggr(0)
            for n in range(2):
                done(dve.memset(wst[:, n], 0.0))
                done(dve.memset(wc[:, n], 0.0))
                done(dve.memset(wa[:, n], 0.0))
            for r in row_bias.values():
                done(dve.memset(r[:].bitcast(F32), 0.0))
            done(dve.memset(ones33[:].bitcast(F32), 1.0))
            done(dve.memset(exp_bias[:], LOG_3_4 - 1.0))
            dve.wait_ge(w_in[3], 16 * (len(small_cols) + 6))
            dve.wait_ge(w_in[0], 64)
            split("wq", 8)
            split("wk", 8)
            split("wv", 8)
            split("wo", None)
            normalise(0, 0)
            dve.wait_ge(w_in[1], 32)
            split("wf1", 10)
            split("wf2", None)
            dve.wait_ge(w_in[2], 32)
            split("w1", 24)
            split("w2", 28)
            dve.wait_ge(s_ident, 6)
            done(dve.tensor_reduce(grp[:], ident[0:ROWS, :].rearrange("p (a b) -> p a b", b=8), AX, ALU.add))
            done(dve.tensor_tensor(sel[:], ident[0:ROWS, 0:H].unsqueeze(2).to_broadcast([ROWS, H, P]),
                                   ident[0:ROWS, 32:32 + H].unsqueeze(2).to_broadcast([ROWS, H, P]), ALU.add))
            settle()
            done(dve.tensor_tensor(grp[:, 8:9], grp[:, 0:1], grp[:, 4:5], ALU.add))
            done(dve.tensor_tensor(grp[:, 9:10], grp[:, 1:2], grp[:, 2:3], ALU.add))
            settle()
            done(dve.tensor_tensor(sgn[:], grp[:, 8:9], grp[:, 9:10], ALU.subtract))
            done(dve.tensor_tensor(grp[:, 10:11], grp[:, 8:9], grp[:, 2:3], ALU.subtract))
            settle()
            done(dve.scalar_tensor_tensor(out=scl[:], in0=grp[:, 10:11], scalar=0.8, in1=grp[:, 1:2], op0=ALU.mult, op1=ALU.add))
            for layer, (name, heads, gain_at) in enumerate((("w1", H, 24), ("w2", 1, 28))):
                w = stage[name]
                for side in range(2):
                    settle()
                    done(dve.tensor_tensor(prod[:], w[:], a_bc[2 * layer + side][:].unsqueeze(1).to_broadcast([P, KT, D]), ALU.mult))
                    settle()
                    done(dve.tensor_reduce(wa[:, layer, side, :, 0:heads], prod[:].rearrange("p k (h d) -> p k h d", h=heads), AX, ALU.add))
                settle()
                for side in range(2):
                    done(dve.tensor_tensor(wag[:, layer, side], wa[:, layer, side],
                                           cols[:, gain_at:gain_at + KT].unsqueeze(2).to_broadcast([P, KT, H]), ALU.mult))
                settle()
                for at, side in ((0, 0), (8, 1), (16, 1), (32, 0), (TROW, 1), (TROW + 8, 1), (TROW + 16, 1)):
                    done(dve.tensor_copy(wst[:, layer, :, at:at + H], wag[:, layer, side]))
                for at in (0, 32):
                    done(dve.tensor_tensor(wc[:, layer, :, at:at + H], wa[:, layer, 0], wa[:, layer, 1], ALU.add))
                settle()
                hi, lo = whl[f"wst{layer + 1}"]
                done(dve.tensor_copy(hi[:], wst[:, layer]))
                settle()
                done(dve.tensor_tensor(lo[:], wst[:, layer], hi[:].bitcast(F32), ALU.subtract))
            setup_at["weights"] = steps[0]
            dve.wait_ge(setup_pe, 1)
            done(dve.tensor_tensor(bcol[:, 0:4], F[0][:, 0:4], cols[:, 2:6], ALU.add))
            done(dve.tensor_tensor(bcol[:, 6:14], F[0][:, 6:14], cols[:, 14:22], ALU.add))
            done(dve.tensor_tensor(bv_col[:], F[0][:, 4:6], cols[:, 6:8], ALU.add))
            for n in range(2):
                done(dve.tensor_copy(cb[n][:], F[0][0:ROWS, 14 + n:15 + n]))
            setup_at["columns"] = steps[0]
            dve.wait_ge(setup_pe, 2)
            done(dve.tensor_tensor(bo_row[:], BK[0:1, 0, 0:D], rows_in[:, 0, :], ALU.add))
            settle()
            for name, src in (("bo", bo_row[:]), ("bf2", rows_in[:, 1, :]), ("c1", BK[0:1, 1, 0:D]), ("c2", BK[0:1, 2, 0:D])):
                done(dve.tensor_copy(row_bias[name][0:1, :], src))
                settle()
                done(dve.tensor_tensor(row_bias[name][32:33, :], src, row_bias[name][0:1, :].bitcast(F32), ALU.subtract))
            settle()
            for r in range(2):
                done(dve.memset(v_sb[r][:], 1.0))
                done(dve.memset(kd_sb[r][:], 0.0))
            setup_at["all"] = steps[0]

            def a_ft_out(i, par):
                dve.wait_ge(a_et, i + 1)
                f = ft_sb[par][:].rearrange("p g n -> p (g n)")
                dve.scalar_tensor_tensor(out=f, in0=F[0][:], scalar=1.0 / 3.0, in1=f, op0=ALU.add, op1=ALU.mult).then_inc(a_ft, 1)

            def a_max(s):
                dve.wait_ge(a_l, s + 1)
                dve.tensor_reduce(mx[:], L_ps, AX, ALU.max).then_inc(a_mx, 1)
                dve.wait_ge(a_mx, s + 1)
                wait_for(dve, a_e, s)
                dve.tensor_scalar(nmx[:], mx[:], -LOGIT_SCALE, None, ALU.mult).then_inc(a_nm, 1)

            def a_norm(s):
                dve.wait_ge(a_o, s + 1)
                dve.tensor_scalar(rsum[:], O_ps[:, :, HD], 1e-6, None, ALU.max).then_inc(a_rs, 1)
                dve.wait_ge(a_rs, s + 1)
                dve.reciprocal(rinv[:], rsum[:]).then_inc(a_ri, 1)
                dve.wait_ge(a_ri, s + 1)
                wait_for(dve, a_at, s)
                dve.tensor_tensor(att[:].rearrange("p (h d) -> p h d", d=HD), O_ps[:, :, 0:HD],
                                  rinv[:].unsqueeze(2).to_broadcast([P, H, HD]), ALU.mult).then_inc(a_att, 1)

            def a_al_out(s):
                dve.wait_ge(a_ah, s + 1)
                dve.tensor_tensor(al[:], WO_ps, ah[:].bitcast(F32), ALU.subtract).then_inc(a_al, 1)

            def a_pt_out(s, par, g):
                dve.wait_ge(a_tt, s + 1)
                wait_for(dve, a_o, s)
                dve.tensor_tensor(pt_sb[:], ET_ps, ft_sb[par][:, g, :].unsqueeze(1).to_broadcast([P, H, P]), ALU.mult).then_inc(a_pt, 1)

            def a_resid(i, g, s):
                dve.wait_ge(a_wo, s + 1)
                dve.tensor_tensor(xs(i, g), WO_ps, xs(i, g), ALU.add).then_inc(a_x, 1)

            def a_ln(i, g, half, par):
                final = isinstance(i, int) and i == NC - 1
                nxt = 0 if final else i + 1
                if g == 1:
                    if final:
                        dve.wait_ge(a_x, G)
                    elif par == 0:
                        dve.wait_ge(x_in[1], (half + 1) * 16)
                    else:
                        dve.wait_ge(x_in[0], (half + 2) * 16)
                    for n in range(G):
                        stats(i + CA + 1, nxt, n)
                    dve.wait_ge(ln_st, (i + CA + 2) * G)
                if g == 2:
                    normalise(i + CA + 1, nxt, (0, 1))
                if g == 3:
                    normalise(i + CA + 1, nxt, (2, 3))

            def a_step(i, half, par):
                first = isinstance(i, int) and i == 0
                for g in range(G):
                    s = i * G + (g - G)
                    prev = not (first or (isinstance(s, int) and s == 0))
                    if g == 0:
                        ln_lo(i + CA)
                    if not first:
                        a_max(s)
                    if not (first or isinstance(s, int) and s < 2):
                        a_resid(*((i - 2, g + 2) if g < 2 else (i - 1, g - 2)), s - 2)
                    if prev:
                        a_norm(s - 1)
                        a_al_out(s - 1)
                    if g == 0:
                        a_ft_out(i, par)
                    a_ln(i, g, half, par)
                    if not first:
                        a_pt_out(s, 1 - par, g)
                    if g == 1:
                        aggr(i + CA + 1)
            chunks(dve, a_step)
            for g in range(G):
                s = (NC - 1) * G + g
                a_max(s)
                a_resid((s - 2) // G, (s - 2) % G, s - 2)
                a_norm(s - 1)
                a_al_out(s - 1)
                a_pt_out(s, (NC - 1) % 2, g)
            a_resid(NC - 1, G - 2, NG - 2)
            a_norm(NG - 1)
            a_al_out(NG - 1)
            a_resid(NC - 1, G - 1, NG - 1)

            def b_step(i, half, par):
                final = isinstance(i, int) and i == NC - 1
                nxt = 0 if final else i + 1
                for f in range(FT):
                    if f == 2:
                        dve.wait_ge(ln_st, (i + CB + 2) * G)
                    dve.wait_ge(b_gh, i * FT + f + 1)
                    dve.tensor_tensor(gl[:, f, :], gf[f % 2][:], gh[:, f, :].bitcast(F32), ALU.subtract).then_inc(b_gl, 1)
                    if f == 0:
                        dve.wait_ge(*((b_x, G) if final else (a_x, (i + 2) * G)))
                    if f < 2:
                        stats(i + CB + 1, nxt, 2 * f)
                        stats(i + CB + 1, nxt, 2 * f + 1)
                    if f == 2:
                        aggr(i + CB + 1)
                    if f == 4:
                        normalise(i + CB + 1, nxt)
                if not final:
                    ln_lo(i + CB + 1)
                for g in range(G):
                    dve.wait_ge(b_o, i * G + g + 1)
                    dve.tensor_tensor(xs(i, g), BK[:, 4 + g % 2, 0:D], xs(i, g), ALU.add).then_inc(b_x, 1)
            ln_lo(CB)
            chunks(dve, b_step)

            def rows_max(e):
                dve.wait_ge(c_st_done, e + 1)
                dve.tensor_reduce(tmx[:], F[1][TROW:TROW + 24, :].rearrange("p (g n) -> p g n", n=P), AX, ALU.max).then_inc(c_rows, 1)
                dve.wait_ge(c_rows, e * 5 + 1)
                dve.tensor_scalar(tms[0:24, :], tmx[:], sgn[0:24, 0:1], None, ALU.mult).then_inc(c_rows, 1)
                dve.tensor_copy(tms[32:40, :], tmx[0:8, :]).then_inc(c_rows, 1)

            def rows_exponent(e, layer):
                dve.wait_ge(c_rows, e * 5 + 3)
                dve.scalar_tensor_tensor(out=u_sb[:].rearrange("p (g n) -> p g n", n=P),
                                         in0=F[1][0:ROWS, :].rearrange("p (g n) -> p g n", n=P), scalar=cb[layer][:, 0:1],
                                         in1=tms[:].unsqueeze(2).to_broadcast([ROWS, G, P]), op0=ALU.add, op1=ALU.add).then_inc(c_rows, 1)
                dve.wait_ge(c_rows, e * 5 + 4)
                dve.tensor_scalar(u_sb[:], u_sb[:], scl[:, 0:1], EXP_LIMIT, ALU.mult, ALU.min).then_inc(c_rows, 1)

            def hb_view(par, layer):
                if layer == 0:
                    return hb[par][:, 0:G * H * HA].rearrange("p (g h c) -> p g h c", g=G, h=H)
                return hb[par][:, 0:G * (D + 1)].rearrange("p (g h c) -> p g h c", g=G, h=1)

            def bq_out(e, par, layer):
                heads = (H, 1)[layer]
                dve.wait_ge(c_bqt, e + 1)
                dve.tensor_copy(bq_sb[par][:], F[1][:].rearrange("p (g c) -> p g c", c=P)[:, :, 0:24]).then_inc(c_bq, 1)
                dve.wait_ge(c_bq, e + 1)
                dve.tensor_copy(hb_view(par, layer)[:, :, :, D // heads], bq_sb[par][:, :, 8:8 + heads]).then_inc(c_one, 1)

            def hb_out(e, par, n):
                dve.wait_ge(c_h, e * 2 + n + 1)
                for g in range(2 * n, 2 * n + 2):
                    r = dve.tensor_tensor(hb_view(par, 0)[:, g, :, 0:HD],
                                          F[n][:, (g % 2) * D:(g % 2 + 1) * D].rearrange("p (h d) -> p h d", h=H),
                                          bq_sb[par][:, g, 8:8 + H].unsqueeze(2).to_broadcast([P, H, HD]), ALU.mult)
                r.then_inc(c_hb, 1)

            def next_stats(i, first, graphs):
                final = isinstance(i, int) and i == NC - 1
                if final and first == CD:
                    return
                if graphs[0] == 0:
                    if first == CD:
                        dve.wait_ge(c_x, (i + 2) * G)
                    else:
                        dve.wait_ge(*((c_x, G) if final else (b_x, (i + 2) * G)))
                for g in graphs:
                    stats(i + first + 1, 0 if final else i + 1, g)

            def rows_max_and_aggr(i, first):
                more = not (isinstance(i, int) and i == NC - 1 and first == CD)
                if more:
                    dve.wait_ge(ln_st, (i + first + 2) * G)
                rows_max(i + (first - CC))
                if more:
                    aggr(i + first + 1)

            def c1_front(i, par, h):
                if h == 0:
                    ln_lo(i + CC)
                if h == 1:
                    next_stats(i, CC, (0, 1))
                if h == 2:
                    next_stats(i, CC, (2, 3))
                if h == 3:
                    rows_max_and_aggr(i, CC)
                if h == 4:
                    rows_exponent(i, 0)
                if h == 6:
                    bq_out(i, par, 0)
                    hb_out(i, par, 0)
                if h == 7:
                    hb_out(i, par, 1)

            def c_scale(i, par, h):
                dve.wait_ge(c_bc, i * H + h + 1)
                dve.wait_ge(c_gt, i + 1)
                wait_for(dve, c_o, i * H + (h - 1))
                for g in range(G):
                    r = dve.scalar_tensor_tensor(out=pp[h % 2][:, g, :], in0=BK[:, h % 2, g * P:(g + 1) * P],
                                                 scalar=bq_sb[par][:, g, 16 + h:17 + h], in1=gt_sb[par][:, g, :],
                                                 op0=ALU.max, op1=ALU.mult)
                r.then_inc(c_pp, 1)

            def c_recip(i):
                dve.wait_ge(c_ev, i * G + G)
                wait_for(dve, c_att, i * G)
                dve.reciprocal(crec[:], o_sb[:].rearrange("p g (h c) -> p g h c", c=HA)[:, :, :, HD]).then_inc(c_rec, 1)

            def c1_step(i, half, par):
                back = not (isinstance(i, int) and i == 0)
                for h in range(H):
                    if back:
                        c_scale(i - 1, 1 - par, h)
                    if h == 0 and back and not (isinstance(i, int) and i == 1):
                        c_recip(i - 2)
                    c1_front(i, par, h)
            dve.wait_ge(b_x, NG)
            dve.memset(tms[:], 0.0).then_inc(c_zero, 1)
            dve.memset(rb[:], 0.0).then_inc(c_zero, 1)
            for r in range(2):
                dve.memset(hb[r][:, G * H * HA:], 0.0).then_inc(c_zero, 1)
            dve.wait_ge(c_zero, 4)
            chunks(dve, c1_step)
            for h in range(H):
                c_scale(NC - 1, (NC - 1) % 2, h)
                if h == 0:
                    c_recip(NC - 2)
            c_recip(NC - 1)

            def d_scale(i, par):
                dve.wait_ge(d_bc, i + 1)
                dve.wait_ge(c_gt, i + NC + 1)
                wait_for(dve, d_o, i * G)
                for g in range(G):
                    dve.scalar_tensor_tensor(out=pp[0][:, g, :], in0=BK[:, 0, g * P:(g + 1) * P],
                                             scalar=bq_sb[par][:, g, 16:17], in1=gt_sb[par][:, g, :],
                                             op0=ALU.max, op1=ALU.mult).then_inc(d_pp, 1)

            def d_recip(i, g):
                dve.wait_ge(d_o, i * G + g + 1)
                dve.reciprocal(crec[:, g, 0:1], BK[:, D_O[g], D:D + 1]).then_inc(d_rec, 1)

            def d_norm(i, half, par, g):
                if g == 0:
                    wait_for(dve, y_out[par], half * 16)
                dve.wait_ge(d_rec, i * G + g + 1)
                dve.scalar_tensor_tensor(out=y_sb[par][:, g, :], in0=BK[:, D_O[g], 0:D], scalar=crec[:, g, 0:1],
                                         in1=xs(i, g), op0=ALU.mult, op1=ALU.add).then_inc(d_y, 1)

            def c2_step(i, half, par):
                back = not (isinstance(i, int) and i == 0)
                if back:
                    d_scale(i - 1, 1 - par)
                ln_lo(i + CD)
                next_stats(i, CD, (0, 1, 2, 3))
                if not (isinstance(i, int) and i == NC - 1):
                    dve.wait_ge(ln_st, (i + CD + 2) * G)
                for g in range(3):
                    if back:
                        d_recip(i - 1, g)
                if not (isinstance(i, int) and i == NC - 1):
                    aggr(i + CD + 1)
                rows_max(i + NC)
                rows_exponent(i + NC, 1)
                prev = (i - 1, half - (1 - par), 1 - par)
                if back:
                    d_norm(*prev, 0)
                    d_norm(*prev, 1)
                bq_out(i + NC, par, 1)
                if back:
                    d_norm(*prev, 2)
                    d_recip(i - 1, 3)
                    d_norm(*prev, 3)
            chunks(dve, c2_step)
            d_scale(NC - 1, 1)
            for g in range(G):
                d_recip(NC - 1, g)
                d_norm(NC - 1, NC // 2 - 1, 1, g)

        @block.sync
        def _(sp):
            def gate(sem, value):
                if isinstance(value, int) and value <= 0:
                    return
                sp.wait_ge(sem, value)
                sp.sem_inc(sp_gates, 1)

            def kp(w):
                return w.rearrange("(k p) n -> p k n", p=P)

            for w, name in ((wq, "wq"), (wk, "wk"), (wv, "wv"), (wo, "wo")):
                sp.dma_start(stage[name][:], kp(w)).then_inc(w_in[0], 16)

            def load_adj(i, half, par):
                sp.dma_start(adj_in[par][:], adj[bass.ds(i * G, G)].rearrange("g p n -> p g n")).then_inc(adj_ld[par], 16)

            def load_a(i, half, par):
                gate(x_in[par], half * 16)
                sp.dma_start(x_all[:, bass.ds(i * G * D, G * D)].rearrange("p (g d) -> p g d", d=D),
                             x[bass.ds(i * G, G)].rearrange("g p d -> p g d")).then_inc(x_in[par], 16)
                gate(adj_t, i - 1)
                load_adj(i, half, par)
                if isinstance(i, int) and i == 0:
                    for w, name in ((wf1, "wf1"), (wf2, "wf2")):
                        sp.dma_start(stage[name][:], kp(w)).then_inc(w_in[1], 16)
                    for w, name in ((w1, "w1"), (w2, "w2")):
                        sp.dma_start(stage[name][:], kp(w)).then_inc(w_in[2], 16)

            def spread_k(i, par):
                gate(a_qkev, i * 4 + 4)
                for g in range(G):
                    gate(a_l, i * G + (g - 1))
                    for r in range(4):
                        rows = slice(HD * r, HD * r + HD)
                        sp.dma_start(kd_sb[g % 2][rows, :, r, :], k_sb[par][rows, :, g * P:(g + 1) * P]).then_inc(kd_ld[g % 2], 16)

            def a_step(i, half, par):
                if not (isinstance(i, int) and i == NC - 1):
                    load_a(i + 1, half + par, 1 - par)
                if not (isinstance(i, int) and i == 0):
                    spread_k(i - 1, 1 - par)
            load_a(0, 0, 0)
            sp.wait_ge(setup_dve, setup_at["all"])
            chunks(sp, a_step)
            spread_k(NC - 1, (NC - 1) % 2)

            for first in (CC, CD):
                def load_c(i, half, par, first=first):
                    gate(adj_t, i + (first - CB - 1))
                    load_adj(i, half, par)
                    if first == CD:
                        store(i, half, par)

                def store(i, half, par):
                    if isinstance(i, int) and i == 0:
                        return
                    gate(d_y, i * G)
                    sp.dma_start(out[bass.ds(i * G - G, G)].rearrange("g p d -> p g d"), y_sb[1 - par][:]).then_inc(y_out[1 - par], 16)
                chunks(sp, load_c)
            gate(d_y, NC * G)
            sp.dma_start(out[(NC - 1) * G:NC * G].rearrange("g p d -> p g d"), y_sb[1][:]).then_inc(y_out[1], 16)
            sp.wait_ge(y_out[0], 16 * (NC // 2))
            sp.wait_ge(y_out[1], 16 * (NC // 2))

        @block.gpsimd
        def _(pool):
            pool.memset(ident[:], 0.0).then_inc(s_ident, 1)
            pool.memset(neg_half[:], -0.5).then_inc(s_ident, 1)
            pool.memset(eps_l0[:], 1e-5).then_inc(s_ident, 1)
            pool.memset(eps_l1[:], 1e-6).then_inc(s_ident, 1)
            pool.memset(zero_g[:], 0.0).then_inc(s_ident, 1)
            pool.wait_ge(s_ident, 5)
            pool.affine_select(out=ident[:], in_=ident[:], compare_op=ALU.not_equal, fill=1.0, base=0,
                               pattern=[[-1, P]], channel_multiplier=1).then_inc(s_ident, 1)

            def rstd_of(c, eps):
                pool.wait_ge(ln_mv, c * G + G)
                pool.tensor_tensor(ve[:], mv[:, :, 1], eps[:], ALU.add).then_inc(ln_ve, 1)
                pool.wait_ge(ln_ve, c + 1)
                pool.tensor_tensor(rstd[:], ve[:], neg_half[:], ALU.pow).then_inc(ln_rs, 1)

            def neg_mean_of(c):
                pool.wait_ge(ln_rs, c + 1)
                pool.tensor_tensor(ve[:], mv[:, :, 0], rstd[:], ALU.mult).then_inc(ln_mr, 1)
                pool.wait_ge(ln_mr, c - CC)
                pool.tensor_tensor(neg_mr[:], zero_g[:], ve[:], ALU.subtract).then_inc(ln_nm, 1)
                pool.wait_ge(ln_nm, c - CC)

            rstd_of(0, EPS[CA])
            for first, last in ((CA, NC - 1), (CB, NC - 1), (CC, NC - 1), (CD, NC - 1)):
                def norms(i, half, par, first=first):
                    final = isinstance(i, int) and i == NC - 1
                    if first == CC and not (isinstance(i, int) and i < 2):
                        residual(i - 2)
                    if not (final and first == CD):
                        if first >= CC:
                            pool.wait_ge(ln_xn, (i + first + 1) * G)
                        rstd_of(i + first + 1, EPS[first + NC] if final else EPS[first])
                        if first >= CC:
                            neg_mean_of(i + first + 1)
                    if first >= CC:
                        rows_lo(i + (first - CC), par)
                def rows_lo(e, par):
                    pool.wait_ge(c_rp, e + 1)
                    pool.tensor_tensor(rp[par][32:40, :], rb[32:40, :], rp[par][32:40, :].bitcast(F32), ALU.subtract).then_inc(c_lo, 1)
                    pool.wait_ge(c_lo, e + 1)

                def residual(i):
                    for g in range(G):
                        pool.wait_ge(c_rec, i + 1)
                        wait_for(pool, c_x, i * G)
                        pool.tensor_tensor(atc[:, g, :].rearrange("p (h d) -> p h d", d=HD),
                                           o_sb[:, g, :].rearrange("p (h c) -> p h c", c=HA)[:, :, 0:HD],
                                           crec[:, g, :].unsqueeze(2).to_broadcast([P, H, HD]), ALU.mult).then_inc(c_att, 1)
                    for g in range(G):
                        pool.wait_ge(c_att, i * G + g + 1)
                        pool.tensor_tensor(xs(i, g), atc[:, g, :], xs(i, g), ALU.add).then_inc(c_x, 1)
                chunks(pool, norms)
                if first == CC:
                    residual(NC - 2)
                    residual(NC - 1)

        @block.scalar
        def _(act):
            for vec, at in small_cols:
                n = vec.shape[0] // P
                with nc.allow_non_contiguous_dma("a vector as columns"):
                    act.dma_start(cols[:, at:at + n], vec.rearrange("(k p) -> p k", p=P)).then_inc(w_in[3], 16)
            for n, a in enumerate((as1, ad1, as2, ad2)):
                act.dma_start(a_bc[n][:], a.rearrange("h k -> (h k)").partition_broadcast(P)).then_inc(w_in[3], 16)
            for n, r in enumerate((bo, bf2)):
                act.dma_start(rows_in[:, n, :], r.rearrange("(a d) -> a d", a=1)).then_inc(w_in[3], 16)

            def ln_hi(c):
                for kt in range(KT):
                    act.wait_ge(ln_t, c * KT + kt + 1)
                    act.activation(xh[:, kt, :], F[kt][:], ACT.Copy).then_inc(ln_xh, 1)

            def a_adj(i, par):
                act.wait_ge(adj_t, i + 1)
                act.activation(ft_sb[par][:].rearrange("p g n -> p (g n)"), F[0][:], ACT.Exp,
                               bias=exp_bias[:, 0:1], scale=2.0).then_inc(a_et, 1)

            def a_qk_out(i, par, n):
                dst = (q_sb, k_sb)[n // 2][par][:, n % 2, :]
                act.wait_ge(a_qk, i * 4 + n + 1)
                act.activation(dst, F[(n + 1) % 2][:], ACT.Identity, bias=bcol[:, n:n + 1]).then_inc(a_qkev, 1)

            def a_v_out(i, par, n):
                act.wait_ge(a_v, i * 2 + n + 1)
                for e in range(2):
                    r = act.activation(v_sb[par][:, (2 * n + e) * H * HA:(2 * n + e + 1) * H * HA].rearrange("p (h c) -> p h c", c=HA)[:, :, 0:HD],
                                       F[1 - n][:, e * D:(e + 1) * D].rearrange("p (h c) -> p h c", c=HD), ACT.Copy)
                r.then_inc(a_vev, 1)

            def a_front(i, par, g):
                if g == 0:
                    a_qk_out(i, par, 0)
                if g == 1:
                    a_qk_out(i, par, 2)
                if g == 3:
                    a_v_out(i, par, 0)
                    a_v_out(i, par, 1)

            def a_front_early(i, par, g):
                if g == 0:
                    ln_hi(i + CA)
                    a_adj(i, par)
                if g == 1:
                    a_qk_out(i, par, 1)
                if g == 2:
                    a_qk_out(i, par, 3)

            def a_exps(s):
                act.wait_ge(a_nm, s + 1)
                wait_for(act, a_tt, s)
                for h in range(H):
                    r = act.activation(e_sb[:, h, :], L_ps[:, h, :], ACT.Exp, bias=nmx[:, h:h + 1], scale=LOGIT_SCALE)
                r.then_inc(a_e, 1)

            def a_ah_out(s):
                act.wait_ge(a_at, s + 1)
                act.activation(ah[:], WO_ps, ACT.Copy).then_inc(a_ah, 1)

            def a_step(i, half, par):
                for g in range(G):
                    s = i * G + (g - G)
                    first = isinstance(i, int) and i == 0
                    if g == 0:
                        a_front_early(i, par, g)
                    if not first:
                        a_exps(s)
                    if g > 0:
                        a_front_early(i, par, g)
                    if not (first or (isinstance(s, int) and s == 0)):
                        a_ah_out(s - 1)
                    a_front(i, par, g)
            act.wait_ge(setup_dve, setup_at["all"])
            chunks(act, a_step)
            for g in range(G):
                s = (NC - 1) * G + g
                a_exps(s)
                a_ah_out(s - 1)
            a_ah_out(NG - 1)

            def b_step(i, half, par):
                for f in range(FT):
                    act.wait_ge(b_h, i * FT + f + 1)
                    if f == 0:
                        wait_for(act, b_o, i * G)
                    wait_for(act, b_gl, i * FT + (f - 1))
                    act.activation(gf[f % 2][:], BK[:, f % 4, :], ACT.Gelu, bias=bcol[:, 6 + f:7 + f])
                    act.activation(gh[:, f, :], BK[:, f % 4, :], ACT.Gelu, bias=bcol[:, 6 + f:7 + f]).then_inc(b_gh, 1)
                if not (isinstance(i, int) and i == NC - 1):
                    ln_hi(i + CB + 1)
            ln_hi(CB)
            act.wait_ge(a_x, NG)
            chunks(act, b_step)

            def normalise(i, first, graphs):
                if isinstance(i, int) and i == NC - 1:
                    if first == CD:
                        return
                    nxt = 0
                else:
                    nxt = i + 1
                c = i + first + 1
                act.wait_ge(ln_nm, c - CC)
                act.wait_ge(ln_t, c * KT)
                for g in graphs:
                    act.activation(xn[:, g, :], xs(nxt, g), ACT.Identity, scale=rstd[:, g:g + 1],
                                   bias=neg_mr[:, g:g + 1]).then_inc(ln_xn, 1)

            def c_front(i, par, first):
                c = i + first
                ln_hi(c)
                act.wait_ge(adj_t, c - NC + 1)
                act.activation(gt_sb[par][:].rearrange("p g n -> p (g n)"), F[0][:], ACT.Exp).then_inc(c_gt, 1)
                act.wait_ge(c_rows, (c - CC) * 5 + 5)
                wait_for(act, c_lo, c - CC)
                act.activation(rb[0:ROWS, :], u_sb[:], ACT.Exp).then_inc(c_rb, 1)
                act.activation(rp[par][:], u_sb[:], ACT.Exp).then_inc(c_rp, 1)
                normalise(i, first, range(G))

            def d_hb(i, par):
                e = i + NC
                act.wait_ge(c_bq, e + 1)
                for n in range(2):
                    act.wait_ge(c_h, e * 2 + 1 + n)
                    for g in range(2 * n, 2 * n + 2):
                        r = act.activation(hb[par][:, g * (D + 1):g * (D + 1) + D],
                                           BK[:, 1 + n, (g % 2) * D:(g % 2 + 1) * D],
                                           ACT.Copy, scale=bq_sb[par][:, g, 8:9])
                    r.then_inc(c_hb, 1)

            act.wait_ge(c_zero, 4)

            def c_out_copy(i):
                wait_for(act, c_att, i * G)
                for g in range(G):
                    act.wait_ge(c_o, (i + 1) * H)
                    act.activation(o_sb[:, g, :], BK[:, 2 + g, 0:H * HA], ACT.Copy).then_inc(c_ev, 1)

            def c1_step(i, half, par):
                if not (isinstance(i, int) and i < 2):
                    c_out_copy(i - 2)
                c_front(i, par, CC)
            chunks(act, c1_step)
            c_out_copy(NC - 2)
            c_out_copy(NC - 1)

            def c2_step(i, half, par):
                c_front(i, par, CD)
                d_hb(i, par)
            chunks(act, c2_step)

        @block.tensor
        def _(pe):
            def three(dst, w_hi, w_lo, m_hi, m_lo, start, stop):
                pe.matmul(dst, w_hi, m_hi, start=start, stop=False)
                pe.matmul(dst, w_hi, m_lo, start=False, stop=False)
                return pe.matmul(dst, w_lo, m_hi, start=False, stop=stop)

            def wide(dst, name, at):
                hi, lo = whl[name]
                for kt in range(KT):
                    r = three(dst, hi[:, kt, at:at + P], lo[:, kt, at:at + P], xh[:, kt, :], xl[:, kt, :], kt == 0, kt == KT - 1)
                return r

            def tall(dst, name, g, bias, start):
                hi, lo = whl[name]
                if bias is not None:
                    pe.matmul(dst, ones33[:], row_bias[bias][:], start=start, stop=False, skip_group_check=True)
                for kt in range(KT):
                    n = slice(g * P, (g + 1) * P)
                    pe.matmul(dst, xh[:, kt, n], hi[:, kt, :], start=start and bias is None and kt == 0, stop=False, skip_group_check=True)
                    pe.matmul(dst, xl[:, kt, n], hi[:, kt, :], start=False, stop=False, skip_group_check=True)
                    r = pe.matmul(dst, xh[:, kt, n], lo[:, kt, :], start=False, stop=(kt == KT - 1), skip_group_check=True)
                return r

            def ln_turn(c):
                pe.wait_ge(ln_xn, c * G + G)
                for kt in range(KT):
                    for g in range(G):
                        r = pe.transpose(F[kt][:, g * P:(g + 1) * P], xn[:, g, kt * P:(kt + 1) * P], ident[:])
                    r.then_inc(ln_t, 1)

            pe.wait_ge(setup_dve, setup_at["weights"])
            pe.wait_ge(s_ident, 6)
            col = 0
            for name, b_at, tiles in (("wq", 0, 2), ("wk", 0, 2), ("wv", 0, 2), ("wf1", 12, FT)):
                for m in range(tiles):
                    for kt in range(KT):
                        pe.matmul(F[0][:, col:col + 1], stage[name][:, kt, m * P:(m + 1) * P], cols[:, b_at + kt:b_at + kt + 1],
                                  start=(kt == 0), stop=(kt == KT - 1), skip_group_check=True)
                    col += 1
            for layer, b_at in ((0, 22), (1, 26)):
                for kt in range(KT):
                    r = pe.matmul(F[0][0:ROWS, col:col + 1], wc[:, layer, kt, :], cols[:, b_at + kt:b_at + kt + 1],
                                  start=(kt == 0), stop=(kt == KT - 1), skip_group_check=True)
                col += 1
            r.then_inc(setup_pe, 1)
            pe.wait_ge(setup_dve, setup_at["columns"])
            for bank, name, vec, at in ((0, "wo", bv_col, 0), (1, "w1", cols, 22), (2, "w2", cols, 26)):
                for kt in range(KT):
                    r = pe.matmul(BK[0:1, bank, 0:D], vec[:, at + kt:at + kt + 1], stage[name][:, kt, :],
                                  start=(kt == 0), stop=(kt == KT - 1))
            r.then_inc(setup_pe, 1)
            pe.wait_ge(setup_dve, setup_at["all"])

            def a_proj(i, n):
                wait_for(pe, *(((ln_xl, (i + CA) * KT + 2)), (a_ft, i + 1), (a_qkev, i * 4 + 1), (a_qkev, i * 4 + 2))[n])
                wide(F[(n + 1) % 2][:], ("wq", "wk")[n // 2], (n % 2) * P).then_inc(a_qk, 1)

            def a_vproj(i, g):
                n, e = g // 2, g % 2
                pe.wait_ge(a_qkev, i * 4 + 3 + n)
                r = tall(F[1 - n][:, e * D:(e + 1) * D], "wv", g, None, e == 0)
                if e == 1:
                    r.then_inc(a_v, 1)

            def adj_turn(c, half, par, first):
                before = {CA: 0, CC: NC // 2, CD: NC}[first]
                pe.wait_ge(adj_ld[par], (half + 1 + before) * 16)
                pe.wait_ge(ln_xl, c * KT + 1)
                for g in range(G):
                    r = pe.transpose(F[0][:, g * P:(g + 1) * P], adj_in[par][:, g, :], ident[:])
                r.then_inc(adj_t, 1)

            def a_front_a(i, g):
                for n in ((0,), (1,), (3,), ())[g]:
                    a_proj(i, n)
                if g == 3:
                    a_vproj(i, 1)
                    a_vproj(i, 2)

            def a_front_b(i, g):
                if g == 1:
                    a_proj(i, 2)
                if g == 2:
                    a_vproj(i, 0)
                if g == 3:
                    a_vproj(i, 3)

            def a_logits(s, i, par, g):
                pe.wait_ge(a_qkev, i * 4 + 4)
                wait_for(pe, a_e, s)
                pe.wait_ge(kd_ld[g % 2], (i * 2 + (g // 2 + 1)) * 64)
                for t in range(2):
                    r = pe.matmul(BK[:, t, :], q_sb[par][:, t, g * P:(g + 1) * P], kd_sb[g % 2][:, t].rearrange("p h n -> p (h n)"),
                                  start=True, stop=True)
                r.then_inc(a_l, 1)

            def a_turn(s):
                pe.wait_ge(a_e, s + 1)
                wait_for(pe, a_pt, s)
                for h in range(H):
                    r = pe.transpose(ET_ps[:, h, :], e_sb[:, h, :], ident[:])
                r.then_inc(a_tt, 1)

            def a_av(s, i, par, g):
                pe.wait_ge(a_vev, i * 2 + 2)
                pe.wait_ge(a_pt, s + 1)
                wait_for(pe, a_att, s)
                for h in range(H):
                    r = pe.matmul(head_out(4, h), pt_sb[:, h, :], head_in(v_sb[par], g, h), start=True, stop=True)
                r.then_inc(a_o, 1)

            def a_attn_turn(s):
                pe.wait_ge(a_att, s + 1)
                wait_for(pe, a_x, s)
                for kt in range(KT):
                    r = pe.transpose(BK[:, 5, kt * P:(kt + 1) * P], att[:, kt * P:(kt + 1) * P], ident[:])
                r.then_inc(a_at, 1)

            def a_out(s):
                pe.wait_ge(a_al, s + 1)
                hi, lo = whl["wo"]
                pe.matmul(WO_ps, ones33[:], row_bias["bo"][:], start=True, stop=False)
                for kt in range(KT):
                    n = slice(kt * P, (kt + 1) * P)
                    pe.matmul(WO_ps, ah[:, n], hi[:, kt, :], start=False, stop=False)
                    pe.matmul(WO_ps, al[:, n], hi[:, kt, :], start=False, stop=False)
                    r = pe.matmul(WO_ps, ah[:, n], lo[:, kt, :], start=False, stop=(kt == KT - 1))
                r.then_inc(a_wo, 1)

            def a_step(i, half, par):
                first = isinstance(i, int) and i == 0
                for g in range(G):
                    s = i * G + (g - G)
                    prev = not (first or (isinstance(s, int) and s == 0))
                    if g == 0:
                        wait_for(pe, a_vev, i * 2)
                        ln_turn(i + CA)
                    if not first:
                        a_logits(s, i - 1, 1 - par, g)
                    if not (first or isinstance(s, int) and s < 2):
                        a_out(s - 2)
                    if g == 0:
                        adj_turn(i + CA, half, par, CA)
                    if prev:
                        a_av(s - 1, *((i - 2, par, G - 1) if g == 0 else (i - 1, 1 - par, g - 1)))
                    a_front_a(i, g)
                    if prev:
                        a_attn_turn(s - 1)
                    a_front_b(i, g)
                    if not first:
                        a_turn(s)
            chunks(pe, a_step)
            for g in range(G):
                s = (NC - 1) * G + g
                a_logits(s, NC - 1, (NC - 1) % 2, g)
                a_out(s - 2)
                a_av(s - 1, (s - 1) // G, (s - 1) // G % 2, (s - 1) % G)
                a_attn_turn(s - 1)
                a_turn(s)
            a_out(NG - 2)
            a_av(NG - 1, NC - 1, (NC - 1) % 2, G - 1)
            a_attn_turn(NG - 1)
            a_out(NG - 1)

            def b_step(i, half, par):
                pe.wait_ge(ln_xl, (i + CB) * KT + 2)
                for f in range(FT):
                    wait_for(pe, b_gh, i * FT + (f - 3))
                    wide(BK[:, f % 4, :], "wf1", f * P).then_inc(b_h, 1)
                if not (isinstance(i, int) and i == NC - 1):
                    ln_turn(i + CB + 1)
                hi, lo = whl["wf2"]
                for g in range(G):
                    dst = BK[:, 4 + g % 2, 0:D]
                    n = slice(g * P, (g + 1) * P)
                    wait_for(pe, b_x, i * G + (g - 1))
                    pe.matmul(dst, ones33[:], row_bias["bf2"][:], start=True, stop=False)
                    for f in range(FT):
                        pe.wait_ge(b_gl, i * FT + f + 1)
                        pe.matmul(dst, gh[:, f, n], hi[:, f, :], start=False, stop=False)
                        pe.matmul(dst, gl[:, f, n], hi[:, f, :], start=False, stop=False)
                        r = pe.matmul(dst, gh[:, f, n], lo[:, f, :], start=False, stop=(f == FT - 1))
                    r.then_inc(b_o, 1)
            pe.wait_ge(a_vev, 2 * NC)
            ln_turn(CB)
            pe.wait_ge(a_x, NG)
            chunks(pe, b_step)

            def c_turn(i, first):
                c, e = i + first, i + (first - CC)
                if first == CC or isinstance(i, int) and i == 0:
                    wait_for(pe, c_hb, e * 2)
                else:
                    pe.wait_ge(c_bq, e)
                if isinstance(c, int) and c == CC:
                    pe.wait_ge(ln_xl, c * KT)
                ln_turn(c)

            def c_st(i, first, kt):
                pe.wait_ge(ln_xl, (i + first) * KT + 2)
                hi, lo = whl[("wst1", "wst2")[(first - CC) // NC]]
                r = three(F[1][:], hi[:, kt, :], lo[:, kt, :], xh[:, kt, :], xl[:, kt, :], kt == 0, kt == KT - 1)
                if kt == KT - 1:
                    r.then_inc(c_st_done, 1)

            def c_b_turn(i, first):
                pe.wait_ge(c_rb, i + (first - CC) + 1)
                for g in range(G):
                    r = pe.transpose(F[1][:, g * P:(g + 1) * P], rb[:, g * P:(g + 1) * P], ident[:])
                r.then_inc(c_bqt, 1)

            def c1_front(i, half, par, h):
                if h == 0:
                    c_turn(i, CC)
                if h == 1:
                    adj_turn(i + CC, half, par, CC)
                    c_st(i, CC, 0)
                if h == 2:
                    c_st(i, CC, 1)
                if h == 3:
                    pe.wait_ge(c_gt, i + 1)
                if h == 5:
                    c_b_turn(i, CC)
                if h == 6:
                    pe.wait_ge(c_bq, i + 1)
                if h in (3, 4, 6, 7):
                    g = (3, 4, 6, 7).index(h)
                    r = tall(F[g // 2][:, (g % 2) * D:(g % 2 + 1) * D], "w1", g, "c1", g % 2 == 0)
                    if g % 2 == 1:
                        r.then_inc(c_h, 1)

            def c_bcast(i, par, h):
                pe.wait_ge(c_rp, i + 1)
                pe.wait_ge(c_lo, i + 1)
                wait_for(pe, c_pp, i * H + (h - 1))
                pe.matmul(BK[:, h % 2, :], sel[:, h, :], rp[par][:], start=True, stop=True).then_inc(c_bc, 1)

            def c_av(i, par, h):
                pe.wait_ge(c_pp, i * H + h + 1)
                if h == 0:
                    pe.wait_ge(c_hb, i * 2 + 2)
                    pe.wait_ge(c_one, i + 1)
                for g in range(G):
                    if h == 0:
                        wait_for(pe, c_ev, i * G + (g - G + 1))
                    r = pe.matmul(head_out(2 + g, h), pp[h % 2][:, g, :], head_in(hb[par], g, h), start=True, stop=True)
                r.then_inc(c_o, 1)

            def c1_step(i, half, par):
                back = not (isinstance(i, int) and i == 0)
                if back:
                    c_bcast(i - 1, 1 - par, 0)
                for h in range(H):
                    if back and h < H - 1:
                        c_bcast(i - 1, 1 - par, h + 1)
                    c1_front(i, half, par, h)
                    if back:
                        c_av(i - 1, 1 - par, h)
            pe.wait_ge(b_x, NG)
            chunks(pe, c1_step)
            last = (NC - 1) % 2
            c_bcast(NC - 1, last, 0)
            for h in range(H):
                if h < H - 1:
                    c_bcast(NC - 1, last, h + 1)
                c_av(NC - 1, last, h)

            def d_bcast(i, par):
                pe.wait_ge(c_rp, i + NC + 1)
                pe.wait_ge(c_lo, i + NC + 1)
                wait_for(pe, d_pp, i * G)
                pe.matmul(BK[:, 0, :], sel[:, 0, :], rp[par][:], start=True, stop=True).then_inc(d_bc, 1)

            def d_av(i, par, g):
                if g == 0:
                    pe.wait_ge(c_hb, (i + NC) * 2 + 2)
                    pe.wait_ge(c_one, i + NC + 1)
                pe.wait_ge(d_pp, i * G + g + 1)
                if g == 3:
                    pe.wait_ge(d_y, i * G + 1)
                else:
                    wait_for(pe, d_y, i * G + (g - G + 1 if g else 0))
                pe.matmul(BK[:, D_O[g], 0:D + 1], pp[0][:, g, :], hb[par][:, g * (D + 1):(g + 1) * (D + 1)],
                          start=True, stop=True).then_inc(d_o, 1)

            def d_h(i, g):
                r = tall(BK[:, 1 + g // 2, (g % 2) * D:(g % 2 + 1) * D], "w2", g, "c2", g % 2 == 0)
                if g % 2 == 1:
                    r.then_inc(c_h, 1)

            def c2_step(i, half, par):
                back = not (isinstance(i, int) and i == 0)
                if back:
                    d_bcast(i - 1, 1 - par)
                c_turn(i, CD)
                if back:
                    for g in range(3):
                        d_av(i - 1, 1 - par, g)
                adj_turn(i + CD, half, par, CD)
                for kt in range(KT):
                    c_st(i, CD, kt)
                wait_for(pe, c_hb, (i + NC) * 2)
                for g in range(3):
                    d_h(i, g)
                c_b_turn(i, CD)
                d_h(i, 3)
                if back:
                    d_av(i - 1, 1 - par, 3)
            pe.wait_ge(c_ev, NG)
            chunks(pe, c2_step)
            d_bcast(NC - 1, last)
            for g in range(G):
                d_av(NC - 1, last, g)




_INS = ['x', 'adj', 'L0_gnn_Wq', 'L0_gnn_bq', 'L0_gnn_Wk', 'L0_gnn_bk', 'L0_gnn_Wv', 'L0_gnn_bv', 'L0_gnn_Wo', 'L0_gnn_bo',
        'L0_gnn_g1', 'L0_gnn_b1', 'L0_gnn_g2', 'L0_gnn_b2', 'L0_gnn_Wf1', 'L0_gnn_bf1', 'L0_gnn_Wf2', 'L0_gnn_bf2',
        'L1_gnn_W1', 'L1_gnn_a_src1', 'L1_gnn_a_dst1', 'L1_gnn_g1', 'L1_gnn_b1',
        'L1_gnn_W2', 'L1_gnn_a_src2', 'L1_gnn_a_dst2', 'L1_gnn_g2', 'L1_gnn_b2']


def kernel(**inputs):
    import numpy as _np
    import concourse.bacc as _bacc
    from concourse import mybir as _mybir
    from concourse.bass_utils import run_bass_kernel_spmd as _run

    nc = _bacc.Bacc("TRN2", target_bir_lowering=False, num_devices=1)
    arrays, args = {}, []
    for name in _INS:
        a = _np.ascontiguousarray(inputs[name])
        arrays[f"in_{name}_dram"] = a
        args.append(nc.dram_tensor(f"in_{name}_dram", a.shape, _mybir.dt.from_np(a.dtype), kind="ExternalInput").ap())
    args.append(nc.dram_tensor("out_0_dram", inputs["x"].shape, _mybir.dt.float32, kind="ExternalOutput").ap())
    build(nc, *args)
    r = _run(nc, [arrays], core_ids=[0])
    return r.results[0]["out_0_dram"]
```

```python
from contextlib import ExitStack

import concourse.bass as bass
from concourse import mybir

F32 = mybir.dt.float32
F32R = mybir.dt.float32r
ALU = mybir.AluOpType
ACT = mybir.ActivationFunctionType
AX = mybir.AxisListType.X

P = 128
D = 256
KT = D // P
G = 4
W4 = G * P
H = 8
HD = D // H
HA = HD + 1
FF = 4 * D
FT = FF // P
LOGIT_SCALE = HD ** -0.5
LOG_3_4 = -0.2876820724517809
EXP_LIMIT = 66.0
AVW = 96
ROWS = 40
TROW = 96


def wait_for(eng, sem, value):
    if isinstance(value, int) and value <= 0:
        return
    eng.wait_ge(sem, value)


def build(nc, x, adj, wq, bq, wk, bk, wv, bv, wo, bo, g1, b1, g2, b2, wf1, bf1, wf2, bf2,
          w1, as1, ad1, lg1, lb1, w2, as2, ad2, lg2, lb2, out):
    NG = x.shape[0]
    NC = NG // G
    assert x.shape[1:] == (P, D) and NC >= 4 and NC % 2 == 0

    ctx = ExitStack()
    with ctx:
        def sb(name, shape, dt=F32):
            return ctx.enter_context(nc.sbuf_tensor(name, shape, dt))

        def sem(name):
            return ctx.enter_context(nc.semaphore(name))

        def psum(name):
            return ctx.enter_context(nc.psum_tensor(name, [P, 512], F32))

        base_of_x = (nc.sbuf_base + 31) // 32 * 32
        x_all = sb("x_all", [P, NG * D])
        adj_in = [sb(f"adj_in{r}", [P, G, P]) for r in range(2)]
        ident = sb("ident", [P, P])
        neg_half = sb("neg_half", [P, G])
        zero_g = sb("zero_g", [P, G])
        eps_l0 = sb("eps_l0", [P, G])
        eps_l1 = sb("eps_l1", [P, G])
        whl = {}
        for name, kt, n in (("wq", KT, D), ("wk", KT, D), ("wv", KT, D), ("wo", KT, D), ("wf1", KT, FF),
                            ("wf2", FT, D), ("w1", KT, D), ("w2", KT, D), ("wst1", KT, P), ("wst2", KT, P)):
            whl[name] = [sb(f"{name}_{part}", [P, kt, n], F32R) for part in ("hi", "lo")]
        bo_bc, bf2_bc, c1_bc, c2_bc = (sb(n, [P, D]) for n in ("bo_bc", "bf2_bc", "c1_bc", "c2_bc"))
        warm = sb("warm", [P, G])
        cols = sb("cols", [P, 40])
        bcol = sb("bcol", [P, 14])
        sel = sb("sel", [ROWS, H, P], F32R)
        sgn = sb("sgn", [ROWS, 1])
        scl = sb("scl", [ROWS, 1])
        cb = [sb(f"cb{n}", [ROWS, 1]) for n in range(2)]
        exp_bias = sb("exp_bias", [P, 1])
        st = sb("st", [P, G, 6])
        mv = sb("mv", [P, G, 2])
        ve = sb("ve", [P, G])
        rstd = sb("rstd", [P, G])
        neg_mr = sb("neg_mr", [P, G])
        xn = sb("xn", [P, G, D])
        xh = sb("xh", [P, KT, W4], F32R)
        xl = sb("xl", [P, KT, W4], F32R)

        REGION = 52 * 1024
        base_of_region = (nc.sbuf_base + 31) // 32 * 32
        sb("region", [P, REGION // 4 + 8])

        def overlay(base, limit):
            at = [base]

            def alloc(name, shape, dt=F32):
                t = nc.alloc_sbuf_tensor_at(name, shape, dt, offset=at[0])
                n = 4
                for d in shape[1:]:
                    n *= d
                at[0] += (n + 31) // 32 * 32
                assert at[0] <= limit, name
                return t
            return alloc

        o = overlay(base_of_x + NG * D * 2, base_of_x + NG * D * 4)
        stage = {"wq": o("s_wq", [P, KT, D]), "wk": o("s_wk", [P, KT, D]), "wv": o("s_wv", [P, KT, D]),
                 "wo": o("s_wo", [P, KT, D]), "wf1": o("s_wf1", [P, KT, FF]), "wf2": o("s_wf2", [P, FT, D]),
                 "w1": o("s_w1", [P, KT, D]), "w2": o("s_w2", [P, KT, D])}
        a_bc = [o(f"a_bc{n}", [P, D]) for n in range(4)]
        o = overlay(base_of_x + 3 * G * D * 4, base_of_x + NG * D * 2)
        scaled = {"wf1": o("wf1_g", [P, KT, FF]), "w1": o("w1_g", [P, KT, D]), "w2": o("w2_g", [P, KT, D])}
        prod = o("prod", [P, KT, D])
        wa = o("wa", [P, 2, 2, KT, H])
        wag = o("wag", [P, 2, 2, KT, H])
        wst = o("wst", [P, 2, KT, P])
        wc = o("wc", [P, 2, KT, ROWS])
        grp = o("grp", [ROWS, 16])
        bv_col = o("bv_col", [P, KT])

        o = overlay(base_of_region, base_of_region + REGION)
        q_sb = [o(f"q{r}", [P, 2, W4]) for r in range(2)]
        k_sb = [o(f"k{r}", [P, 2, W4]) for r in range(2)]
        kd_sb = [o(f"kd{r}", [P, 2, 4, P]) for r in range(2)]
        v_sb = [o(f"v{r}", [P, G * H * HA + AVW - HA]) for r in range(2)]
        ft_sb = [o(f"ft{r}", [P, G, P]) for r in range(2)]
        e_sb = o("e_sb", [P, H, P])
        pt_sb = o("pt_sb", [P, H, P])
        att = o("att", [P, D])
        ah = o("ah", [P, D], F32R)
        al = o("al", [P, D], F32R)
        mx = o("mx", [P, H])
        nmx = o("nmx", [P, H])
        rsum = o("rsum", [P, H])
        rinv = o("rinv", [P, H])
        b_wide = [o(f"b_wide{n}", [P, KT, P]) for n in range(3)]

        o = overlay(base_of_region, base_of_region + REGION)
        gh = o("gh", [P, FT, W4], F32R)
        gl = o("gl", [P, FT, W4], F32R)
        gf = [o(f"gf{r}", [P, W4]) for r in range(2)]

        o = overlay(base_of_region, base_of_region + REGION)
        gt_sb = [o(f"gt{r}", [P, G, P]) for r in range(2)]
        hb = [o(f"hb{r}", [P, G * H * HA + AVW - HA]) for r in range(2)]
        bq_sb = [o(f"bqs{r}", [P, G, 24]) for r in range(2)]
        rp = [o(f"rp{r}", [ROWS, W4], F32R) for r in range(2)]
        tmx = o("tmx", [24, G])
        tms = o("tms", [ROWS, G])
        u_sb = o("u_sb", [ROWS, W4])
        rb = o("rb", [P, W4])
        pp = [o(f"pp{r}", [P, G, P]) for r in range(2)]
        o_sb = o("o_sb", [P, G, H * HA])
        atc = o("atc", [P, G, D])
        crec = o("crec", [P, G, H])
        y_sb = [o(f"y{r}", [P, G, D]) for r in range(2)]

        F = [psum("F0"), psum("F1")]
        BK = ctx.enter_context(nc.psum_tensor("BK", [P, 6, 512], F32))
        L_ps = BK[:, 0:2, :].rearrange("p a (h n) -> p (a h) n", n=P)
        ET_ps = BK[:, 2:4, :].rearrange("p a (h n) -> p (a h) n", n=P)
        O_ps = BK[:, 4, 0:H * HA].rearrange("p (h c) -> p h c", c=HA)

        D_O = (3, 4, 5, 3)

        def head_out(bank, h):
            return BK[:, bank, h * HA:h * HA + AVW]

        def head_in(t, g, h):
            return t[:, (g * H + h) * HA:(g * H + h) * HA + AVW]

        WO_ps = BK[:, 5, 0:D]

        w_in = [sem("w_in_qkvo"), sem("w_in_ff"), sem("w_in_l1"), sem("w_in_cols"), sem("w_in_rows")]
        s_ident = sem("s_ident")
        setup_dve = sem("setup_dve")
        setup_pe = sem("setup_pe")
        setup_act = sem("setup_act")
        setup_pool = sem("setup_pool")
        s_clear = sem("s_clear")
        x_in = [sem("x_in0"), sem("x_in1")]
        adj_ld = [sem("adj_ld0"), sem("adj_ld1")]
        ln_st, ln_mv, ln_ve, ln_rs, ln_xn, ln_t, ln_xh, ln_xl = (
            sem(n) for n in ("ln_st", "ln_mv", "ln_ve", "ln_rs", "ln_xn", "ln_t", "ln_xh", "ln_xl"))
        ln_mr = sem("ln_mr")
        ln_nm = sem("ln_nm")
        adj_t = sem("adj_t")
        sp_gates = sem("sp_gates")
        kd_ld = [sem("kd_ld0"), sem("kd_ld1")]
        a_et, a_ft, a_qk, a_qkev, a_v, a_vev = (sem(n) for n in ("a_et", "a_ft", "a_qk", "a_qkev", "a_v", "a_vev"))
        a_l, a_mx, a_nm, a_e, a_tt, a_pt, a_o, a_rs, a_ri, a_att, a_at, a_ah, a_al, a_wo, a_x = (
            sem(n) for n in ("a_l", "a_mx", "a_nm", "a_e", "a_tt", "a_pt", "a_o", "a_rs", "a_ri", "a_att",
                             "a_at", "a_ah", "a_al", "a_wo", "a_x"))
        a_xb = sem("a_xb")
        b_xb = sem("b_xb")
        c_xb, d_xb = sem("c_xb"), sem("d_xb")
        b_h, b_gh, b_gl, b_o, b_x = (sem(n) for n in ("b_h", "b_gh", "b_gl", "b_o", "b_x"))
        c_gt, c_st_done, c_rows, c_rb, c_bqt, c_bq, c_h, c_hb, c_one, c_zero = (
            sem(n) for n in ("c_gt", "c_st_done", "c_rows", "c_rb", "c_bqt", "c_bq", "c_h", "c_hb", "c_one", "c_zero"))
        c_rp, c_lo = sem("c_rp"), sem("c_lo")
        c_bc, c_pp, c_o, c_ev, c_rec, c_att, c_x = (sem(n) for n in ("c_bc", "c_pp", "c_o", "c_ev", "c_rec", "c_att", "c_x"))
        d_bc, d_pp, d_o, d_rec, d_y = (sem(n) for n in ("d_bc", "d_pp", "d_o", "d_rec", "d_y"))
        y_out = [sem("y_out0"), sem("y_out1")]
        C_START, Y_START = 1, 16

        CA, CB, CC, CD = 0, NC, 2 * NC, 3 * NC
        EPS = {CA: eps_l0, CB: eps_l0, CC: eps_l1, CD: eps_l1}

        def xs(i, g):
            return x_all[:, bass.ds((i * G + g) * D, D)]

        def chunks(eng, step, n=NC):
            for i in range(2):
                step(i, 0, i)
            with eng.Fori(1, n // 2 - 1) as t:
                step(t * 2, t, 0)
                step(t * 2 + 1, t, 1)
            for i in range(n - 2, n):
                step(i, n // 2 - 1, i % 2)

        FF_L1 = (("wf1", 10), ("wf2", None), ("w1", 24), ("w2", 28))
        setup_act_steps = len(FF_L1)
        setup_pool_steps = 2 * len(FF_L1) - 1
        setup_at = {}
        block = ctx.enter_context(nc.Block())

        small_cols = [(b1, 0), (bq, 2), (bk, 4), (bv, 6), (g1, 8), (g2, 10), (b2, 12), (bf1, 14),
                      (lb1, 22), (lg1, 24), (lb2, 26), (lg2, 28)]

        @block.vector
        def _(dve):
            def stats(c, i, g):
                dve.bn_stats(st[:, g, :], xs(i, g)).then_inc(ln_st, 1)

            def aggr(c):
                for g in range(G):
                    dve.bn_aggr(mv[:, g, :], st[:, g, :]).then_inc(ln_mv, 1)

            def normalise(c, i, graphs=range(G)):
                dve.wait_ge(ln_rs, c + 1)
                wait_for(dve, ln_t, c * KT)
                for g in graphs:
                    dve.tensor_scalar(xn[:, g, :], xs(i, g), mv[:, g, 0:1], rstd[:, g:g + 1],
                                      ALU.subtract, ALU.mult).then_inc(ln_xn, 1)

            def ln_lo(c):
                for kt in range(KT):
                    dve.wait_ge(ln_xh, c * KT + kt + 1)
                    dve.tensor_tensor(xl[:, kt, :], F[kt][:], xh[:, kt, :].bitcast(F32), ALU.subtract).then_inc(ln_xl, 1)

            steps = [0]

            def done(ins):
                steps[0] += 1
                ins.then_inc(setup_dve, 1)

            def settle():
                dve.wait_ge(setup_dve, steps[0])

            def split(name, gain_at):
                hi, lo, w = whl[name][0], whl[name][1], stage[name]
                kts = w.shape[1]
                for kt in range(kts):
                    if gain_at is None:
                        done(dve.tensor_copy(hi[:, kt, :], w[:, kt, :]))
                    else:
                        done(dve.tensor_scalar(hi[:, kt, :], w[:, kt, :], cols[:, gain_at + kt:gain_at + kt + 1], None, ALU.mult))
                settle()
                for kt in range(kts):
                    if gain_at is None:
                        done(dve.tensor_tensor(lo[:, kt, :], w[:, kt, :], hi[:, kt, :].bitcast(F32), ALU.subtract))
                    else:
                        done(dve.scalar_tensor_tensor(out=lo[:, kt, :], in0=w[:, kt, :], scalar=cols[:, gain_at + kt:gain_at + kt + 1],
                                                      in1=hi[:, kt, :].bitcast(F32), op0=ALU.mult, op1=ALU.subtract))

            for n in range(2):
                done(dve.memset(wst[:, n], 0.0))
                done(dve.memset(wc[:, n], 0.0))
                done(dve.memset(wa[:, n], 0.0))
            done(dve.memset(exp_bias[:], LOG_3_4 - 1.0))
            dve.wait_ge(x_in[0], 16)
            for g in range(G):
                stats(0, 0, g)
            dve.wait_ge(ln_st, G)
            aggr(0)
            setup_at["constants"] = steps[0]
            normalise(0, 0)
            dve.wait_ge(w_in[3], 16 * len(small_cols))
            dve.wait_ge(w_in[0], 64)
            split("wq", 8)
            split("wk", 8)
            split("wv", 8)
            split("wo", None)
            dve.wait_ge(setup_pe, 1)
            done(dve.tensor_tensor(bcol[:, 0:4], BK[:, 4, 0:4], cols[:, 2:6], ALU.add))
            done(dve.tensor_tensor(bv_col[:], BK[:, 4, 4:6], cols[:, 6:8], ALU.add))
            setup_at["projections"] = steps[0]

            def setup_rows():
                for n, b in enumerate((bv_col[:], cols[:, 22:24], cols[:, 26:28])):
                    done(dve.tensor_copy(b_wide[n][:], b.unsqueeze(2).to_broadcast([P, KT, P])))
                dve.wait_ge(s_ident, 6)
                done(dve.tensor_reduce(grp[:], ident[0:ROWS, :].rearrange("p (a b) -> p a b", b=8), AX, ALU.add))
                done(dve.tensor_tensor(sel[:], ident[0:ROWS, 0:H].unsqueeze(2).to_broadcast([ROWS, H, P]),
                                       ident[0:ROWS, 32:32 + H].unsqueeze(2).to_broadcast([ROWS, H, P]), ALU.add))
                settle()
                done(dve.tensor_tensor(grp[:, 8:9], grp[:, 0:1], grp[:, 4:5], ALU.add))
                done(dve.tensor_tensor(grp[:, 9:10], grp[:, 1:2], grp[:, 2:3], ALU.add))
                settle()
                done(dve.tensor_tensor(sgn[:], grp[:, 8:9], grp[:, 9:10], ALU.subtract))
                done(dve.tensor_tensor(grp[:, 10:11], grp[:, 8:9], grp[:, 2:3], ALU.subtract))
                settle()
                done(dve.scalar_tensor_tensor(out=scl[:], in0=grp[:, 10:11], scalar=0.8, in1=grp[:, 1:2], op0=ALU.mult, op1=ALU.add))
                dve.wait_ge(w_in[2], 32)
                dve.wait_ge(w_in[4], 16 * 6)
                for layer, (name, heads, gain_at) in enumerate((("w1", H, 24), ("w2", 1, 28))):
                    w = stage[name]
                    for side in range(2):
                        settle()
                        done(dve.tensor_tensor(prod[:], w[:], a_bc[2 * layer + side][:].unsqueeze(1).to_broadcast([P, KT, D]), ALU.mult))
                        settle()
                        done(dve.tensor_reduce(wa[:, layer, side, :, 0:heads], prod[:].rearrange("p k (h d) -> p k h d", h=heads), AX, ALU.add))
                    settle()
                    for side in range(2):
                        done(dve.tensor_tensor(wag[:, layer, side], wa[:, layer, side],
                                               cols[:, gain_at:gain_at + KT].unsqueeze(2).to_broadcast([P, KT, H]), ALU.mult))
                    settle()
                    for at, side in ((0, 0), (8, 1), (16, 1), (32, 0), (TROW, 1), (TROW + 8, 1), (TROW + 16, 1)):
                        done(dve.tensor_copy(wst[:, layer, :, at:at + H], wag[:, layer, side]))
                    for at in (0, 32):
                        done(dve.tensor_tensor(wc[:, layer, :, at:at + H], wa[:, layer, 0], wa[:, layer, 1], ALU.add))
                    settle()
                    hi, lo = whl[f"wst{layer + 1}"]
                    done(dve.tensor_copy(hi[:], wst[:, layer]))
                    settle()
                    done(dve.tensor_tensor(lo[:], wst[:, layer], hi[:].bitcast(F32), ALU.subtract))
                setup_at["rows"] = steps[0]

            def setup_biases():
                dve.wait_ge(setup_pe, 2)
                done(dve.tensor_tensor(bo_bc[:], BK[:, 3, 0:D], bo_bc[:], ALU.add))
                done(dve.tensor_tensor(bcol[:, 6:14], BK[:, 4, 6:14], cols[:, 14:22], ALU.add))
                for n in range(2):
                    done(dve.tensor_copy(cb[n][:], BK[0:ROWS, 4, 14 + n:15 + n]))
                done(dve.tensor_copy(c1_bc[:], BK[:, 5, 0:D]))
                done(dve.tensor_copy(c2_bc[:], BK[:, 5, D:2 * D]))
                setup_at["all"] = steps[0]

            def a_ft_out(i, par):
                dve.wait_ge(a_et, i + 1)
                f = ft_sb[par][:].rearrange("p g n -> p (g n)")
                dve.scalar_tensor_tensor(out=f, in0=F[0][:], scalar=1.0 / 3.0, in1=f, op0=ALU.add, op1=ALU.mult).then_inc(a_ft, 1)

            def a_max(s):
                dve.wait_ge(a_l, s + 1)
                dve.tensor_reduce(mx[:], L_ps, AX, ALU.max).then_inc(a_mx, 1)
                dve.wait_ge(a_mx, s + 1)
                wait_for(dve, a_e, s)
                dve.tensor_scalar(nmx[:], mx[:], -LOGIT_SCALE, None, ALU.mult).then_inc(a_nm, 1)

            def a_norm(s):
                dve.wait_ge(a_o, s + 1)
                dve.tensor_scalar(rsum[:], O_ps[:, :, HD], 1e-6, None, ALU.max).then_inc(a_rs, 1)
                dve.wait_ge(a_rs, s + 1)
                dve.reciprocal(rinv[:], rsum[:]).then_inc(a_ri, 1)
                dve.wait_ge(a_ri, s + 1)
                wait_for(dve, a_at, s)
                dve.tensor_tensor(att[:].rearrange("p (h d) -> p h d", d=HD), O_ps[:, :, 0:HD],
                                  rinv[:].unsqueeze(2).to_broadcast([P, H, HD]), ALU.mult).then_inc(a_att, 1)

            def a_al_out(s):
                dve.wait_ge(a_ah, s + 1)
                dve.tensor_tensor(al[:], WO_ps, ah[:].bitcast(F32), ALU.subtract).then_inc(a_al, 1)

            def a_pt_out(s, par, g):
                dve.wait_ge(a_tt, s + 1)
                wait_for(dve, a_o, s)
                dve.tensor_tensor(pt_sb[:], ET_ps, ft_sb[par][:, g, :].unsqueeze(1).to_broadcast([P, H, P]), ALU.mult).then_inc(a_pt, 1)

            def a_resid(i, g, s):
                dve.wait_ge(a_wo, s + 1)
                dve.wait_ge(a_xb, i * G + g + 1)
                dve.tensor_tensor(xs(i, g), WO_ps, xs(i, g), ALU.add).then_inc(a_x, 1)

            def a_ln(i, g, half, par):
                final = isinstance(i, int) and i == NC - 1
                nxt = 0 if final else i + 1
                if g == 1:
                    if final:
                        dve.wait_ge(a_x, G)
                    elif par == 0:
                        dve.wait_ge(x_in[1], (half + 1) * 16)
                    else:
                        dve.wait_ge(x_in[0], (half + 2) * 16)
                    for n in range(G):
                        stats(i + CA + 1, nxt, n)
                    dve.wait_ge(ln_st, (i + CA + 2) * G)
                if g == 2:
                    normalise(i + CA + 1, nxt, (0, 1))
                if g == 3:
                    normalise(i + CA + 1, nxt, (2, 3))

            def a_step(i, half, par):
                first = isinstance(i, int) and i == 0
                for g in range(G):
                    s = i * G + (g - G)
                    prev = not (first or (isinstance(s, int) and s == 0))
                    if g == 0:
                        ln_lo(i + CA)
                    if not first:
                        a_max(s)
                    if not (first or isinstance(s, int) and s < 2):
                        a_resid(*((i - 2, g + 2) if g < 2 else (i - 1, g - 2)), s - 2)
                    if prev:
                        a_norm(s - 1)
                        a_al_out(s - 1)
                    if g == 0:
                        a_ft_out(i, par)
                        if first:
                            setup_rows()
                    a_ln(i, g, half, par)
                    if not first:
                        a_pt_out(s, 1 - par, g)
                    if g == 1:
                        aggr(i + CA + 1)
                if first:
                    setup_biases()
            chunks(dve, a_step)
            ln_lo(CB)
            for g in range(G):
                s = (NC - 1) * G + g
                a_max(s)
                a_resid((s - 2) // G, (s - 2) % G, s - 2)
                a_norm(s - 1)
                a_al_out(s - 1)
                a_pt_out(s, (NC - 1) % 2, g)
            a_resid(NC - 1, G - 2, NG - 2)
            a_norm(NG - 1)
            a_al_out(NG - 1)
            a_resid(NC - 1, G - 1, NG - 1)

            def b_step(i, half, par):
                final = isinstance(i, int) and i == NC - 1
                nxt = 0 if final else i + 1
                for f in range(FT):
                    if f == 2:
                        dve.wait_ge(ln_st, (i + CB + 2) * G)
                    dve.wait_ge(b_gh, i * FT + f + 1)
                    dve.tensor_tensor(gl[:, f, :], gf[f % 2][:], gh[:, f, :].bitcast(F32), ALU.subtract).then_inc(b_gl, 1)
                    if f == 0:
                        dve.wait_ge(*((b_x, G) if final else (a_x, (i + 2) * G)))
                    if f < 2:
                        stats(i + CB + 1, nxt, 2 * f)
                        stats(i + CB + 1, nxt, 2 * f + 1)
                    if f == 2:
                        aggr(i + CB + 1)
                    if f == 4:
                        normalise(i + CB + 1, nxt)
                ln_lo(i + CB + 1)
                for g in range(G):
                    dve.wait_ge(b_o, i * G + g + 1)
                    dve.wait_ge(b_xb, i * G + g + 1)
                    dve.tensor_tensor(xs(i, g), BK[:, 4 + g % 2, 0:D], xs(i, g), ALU.add).then_inc(b_x, 1)
            chunks(dve, b_step)

            def rows_max(e):
                dve.wait_ge(c_st_done, e + 1)
                dve.tensor_reduce(tmx[:], F[1][TROW:TROW + 24, :].rearrange("p (g n) -> p g n", n=P), AX, ALU.max).then_inc(c_rows, 1)
                dve.wait_ge(c_rows, e * 5 + 1)
                dve.tensor_scalar(tms[0:24, :], tmx[:], sgn[0:24, 0:1], None, ALU.mult).then_inc(c_rows, 1)
                dve.tensor_copy(tms[32:40, :], tmx[0:8, :]).then_inc(c_rows, 1)

            def rows_exponent(e, layer):
                dve.wait_ge(c_rows, e * 5 + 3)
                dve.scalar_tensor_tensor(out=u_sb[:].rearrange("p (g n) -> p g n", n=P),
                                         in0=F[1][0:ROWS, :].rearrange("p (g n) -> p g n", n=P), scalar=cb[layer][:, 0:1],
                                         in1=tms[:].unsqueeze(2).to_broadcast([ROWS, G, P]), op0=ALU.add, op1=ALU.add).then_inc(c_rows, 1)
                dve.wait_ge(c_rows, e * 5 + 4)
                dve.tensor_scalar(u_sb[:], u_sb[:], scl[:, 0:1], EXP_LIMIT, ALU.mult, ALU.min).then_inc(c_rows, 1)

            def hb_view(par, layer):
                if layer == 0:
                    return hb[par][:, 0:G * H * HA].rearrange("p (g h c) -> p g h c", g=G, h=H)
                return hb[par][:, 0:G * (D + 1)].rearrange("p (g h c) -> p g h c", g=G, h=1)

            def bq_out(e, par, layer):
                heads = (H, 1)[layer]
                dve.wait_ge(c_bqt, e + 1)
                dve.tensor_copy(bq_sb[par][:], F[1][:].rearrange("p (g c) -> p g c", c=P)[:, :, 0:24]).then_inc(c_bq, 1)
                dve.wait_ge(c_bq, e + 1)
                dve.tensor_copy(hb_view(par, layer)[:, :, :, D // heads], bq_sb[par][:, :, 8:8 + heads]).then_inc(c_one, 1)

            def hb_out(e, par, n):
                dve.wait_ge(c_h, e * 2 + n + 1)
                for g in range(2 * n, 2 * n + 2):
                    r = dve.tensor_tensor(hb_view(par, 0)[:, g, :, 0:HD],
                                          F[n][:, (g % 2) * D:(g % 2 + 1) * D].rearrange("p (h d) -> p h d", h=H),
                                          bq_sb[par][:, g, 8:8 + H].unsqueeze(2).to_broadcast([P, H, HD]), ALU.mult)
                r.then_inc(c_hb, 1)

            def next_stats(i, graphs):
                final = isinstance(i, int) and i == NC - 1
                if graphs[0] == 0:
                    dve.wait_ge(*((c_x, C_START + G) if final else (b_x, (i + 2) * G)))
                for g in graphs:
                    stats(i + CC + 1, 0 if final else i + 1, g)

            def rows_max_and_aggr(i, first):
                more = not (isinstance(i, int) and i == NC - 1 and first == CD)
                if more:
                    dve.wait_ge(ln_st, (i + first + 2) * G)
                rows_max(i + (first - CC))
                if more:
                    aggr(i + first + 1)

            def c1_front(i, par, h):
                if h == 1:
                    if not (isinstance(i, int) and i == 0):
                        ln_lo(i + CC)
                    next_stats(i, (0, 1))
                if h == 2:
                    next_stats(i, (2, 3))
                if h == 3:
                    rows_max_and_aggr(i, CC)
                if h == 4:
                    rows_exponent(i, 0)
                if h == 6:
                    bq_out(i, par, 0)
                    hb_out(i, par, 0)
                if h == 7:
                    hb_out(i, par, 1)

            def c_scale(i, par, h):
                dve.wait_ge(c_bc, i * H + h + 1)
                dve.wait_ge(c_gt, i + 1)
                wait_for(dve, c_o, i * H + (h - 1))
                for g in range(G):
                    r = dve.scalar_tensor_tensor(out=pp[h % 2][:, g, :], in0=BK[:, h % 2, g * P:(g + 1) * P],
                                                 scalar=bq_sb[par][:, g, 16 + h:17 + h], in1=gt_sb[par][:, g, :],
                                                 op0=ALU.max, op1=ALU.mult)
                r.then_inc(c_pp, 1)

            def c_recip(i):
                dve.wait_ge(c_ev, i * G + G)
                wait_for(dve, c_att, i * G + C_START)
                dve.reciprocal(crec[:], o_sb[:].rearrange("p g (h c) -> p g h c", c=HA)[:, :, :, HD]).then_inc(c_rec, 1)

            def c1_step(i, half, par):
                back = not (isinstance(i, int) and i == 0)
                for h in range(H):
                    if back:
                        c_scale(i - 1, 1 - par, h)
                    c1_front(i, par, h)
                    if h == 1 and back and not (isinstance(i, int) and i == 1):
                        c_recip(i - 2)
            dve.wait_ge(b_x, NG)
            dve.memset(tms[:], 0.0).then_inc(c_zero, 1)
            dve.memset(rb[:], 0.0).then_inc(c_zero, 1)
            for r in range(2):
                dve.memset(hb[r][:, G * H * HA:], 0.0).then_inc(c_zero, 1)
            dve.wait_ge(c_zero, 4)
            chunks(dve, c1_step)
            for h in range(H):
                c_scale(NC - 1, (NC - 1) % 2, h)
                if h == 0:
                    c_recip(NC - 2)
            c_recip(NC - 1)

            def d_scale(i, par):
                dve.wait_ge(d_bc, i + 1)
                dve.wait_ge(c_gt, i + NC + 1)
                wait_for(dve, d_o, i * G)
                for g in range(G):
                    dve.scalar_tensor_tensor(out=pp[0][:, g, :], in0=BK[:, 0, g * P:(g + 1) * P],
                                             scalar=bq_sb[par][:, g, 16:17], in1=gt_sb[par][:, g, :],
                                             op0=ALU.max, op1=ALU.mult).then_inc(d_pp, 1)

            def d_recip(i, g):
                dve.wait_ge(d_o, i * G + g + 1)
                dve.reciprocal(crec[:, g, 0:1], BK[:, D_O[g], D:D + 1]).then_inc(d_rec, 1)

            def d_norm(i, half, par, g):
                if g == 0:
                    dve.wait_ge(y_out[par], half * 16 + Y_START)
                dve.wait_ge(d_rec, i * G + g + 1)
                dve.wait_ge(d_xb, i * G + g + 1)
                dve.scalar_tensor_tensor(out=y_sb[par][:, g, :], in0=BK[:, D_O[g], 0:D], scalar=crec[:, g, 0:1],
                                         in1=xs(i, g), op0=ALU.mult, op1=ALU.add).then_inc(d_y, 1)

            def c2_step(i, half, par):
                back = not (isinstance(i, int) and i == 0)
                more = not (isinstance(i, int) and i == NC - 1)
                ln_lo(i + CD)
                if back:
                    d_scale(i - 1, 1 - par)
                if more:
                    for g in range(2 if back else 0, G):
                        if not back and g == 0:
                            dve.wait_ge(c_x, C_START + NG)
                        stats(i + CD + 1, i + 1, g)
                rows_max_and_aggr(i, CD)
                rows_exponent(i + NC, 1)
                for g in range(3):
                    if back:
                        d_recip(i - 1, g)
                prev = (i - 1, half - (1 - par), 1 - par)
                if more:
                    normalise(i + CD + 1, i + 1, (3,))
                if back:
                    d_norm(*prev, 0)
                early = not (isinstance(i, int) and i >= NC - 2)
                if early:
                    stats(i + CD + 2, i + 2, 0)
                bq_out(i + NC, par, 1)
                if back:
                    d_norm(*prev, 1)
                    d_norm(*prev, 2)
                    d_recip(i - 1, 3)
                    d_norm(*prev, 3)
                if early:
                    stats(i + CD + 2, i + 2, 1)
            chunks(dve, c2_step)
            d_scale(NC - 1, 1)
            for g in range(G):
                d_recip(NC - 1, g)
                d_norm(NC - 1, NC // 2 - 1, 1, g)

        @block.sync
        def _(sp):
            def gate(sem, value):
                if isinstance(value, int) and value <= 0:
                    return
                sp.wait_ge(sem, value)
                sp.sem_inc(sp_gates, 1)

            def kp(w):
                return w.rearrange("(k p) n -> p k n", p=P)

            for w, name in ((wq, "wq"), (wk, "wk"), (wv, "wv"), (wo, "wo")):
                sp.dma_start(stage[name][:], kp(w)).then_inc(w_in[0], 16)

            def load_adj(i, half, par):
                sp.dma_start(adj_in[par][:], adj[bass.ds(i * G, G)].rearrange("g p n -> p g n")).then_inc(adj_ld[par], 16)

            def load_a(i, half, par):
                gate(x_in[par], half * 16)
                sp.dma_start(x_all[:, bass.ds(i * G * D, G * D)].rearrange("p (g d) -> p g d", d=D),
                             x[bass.ds(i * G, G)].rearrange("g p d -> p g d")).then_inc(x_in[par], 16)
                gate(adj_t, i - 1)
                load_adj(i, half, par)
                if isinstance(i, int) and i == 0:
                    sp.wait_ge(w_in[3], 16 * len(small_cols))
                    for w, name in ((w1, "w1"), (w2, "w2")):
                        sp.dma_start(stage[name][:], kp(w)).then_inc(w_in[2], 16)
                    for w, name in ((wf1, "wf1"), (wf2, "wf2")):
                        sp.dma_start(stage[name][:], kp(w)).then_inc(w_in[1], 16)

            def spread_k(i, par):
                gate(a_qkev, i * 4 + 4)
                for g in range(G):
                    gate(a_l, i * G + (g - 1))
                    for r in range(4):
                        rows = slice(HD * r, HD * r + HD)
                        sp.dma_start(kd_sb[g % 2][rows, :, r, :], k_sb[par][rows, :, g * P:(g + 1) * P]).then_inc(kd_ld[g % 2], 16)

            def a_step(i, half, par):
                if not (isinstance(i, int) and i == NC - 1):
                    load_a(i + 1, half + par, 1 - par)
                if not (isinstance(i, int) and i == 0):
                    spread_k(i - 1, 1 - par)
                if isinstance(i, int) and i == 1:
                    sp.wait_ge(setup_dve, setup_at["all"])
                    sp.wait_ge(setup_act, setup_act_steps)
                    sp.wait_ge(setup_pool, setup_pool_steps)
                    sp.wait_ge(setup_pe, 2)
            for r in range(2):
                sp.sem_inc(y_out[r], Y_START)
            load_a(0, 0, 0)
            sp.wait_ge(s_clear, 4)
            chunks(sp, a_step)
            spread_k(NC - 1, (NC - 1) % 2)

            def load_c(i, par, first):
                gate(adj_t, i + (first - CB - 1))
                sp.dma_start(adj_in[par][:], adj[bass.ds(i * G, G)].rearrange("g p n -> p g n")).then_inc(adj_ld[par], 16)

            def c1_step(i, half, par):
                if not (isinstance(i, int) and i == NC - 1):
                    load_c(i + 1, 1 - par, CC)

            def c2_step(i, half, par):
                if not (isinstance(i, int) and i == NC - 1):
                    load_c(i + 1, 1 - par, CD)
                if not (isinstance(i, int) and i == 0):
                    gate(d_y, i * G)
                    sp.dma_start(out[bass.ds(i * G - G, G)].rearrange("g p d -> p g d"), y_sb[1 - par][:]).then_inc(y_out[1 - par], 16)
            load_c(0, 0, CC)
            chunks(sp, c1_step)
            load_c(0, 0, CD)
            chunks(sp, c2_step)
            gate(d_y, NC * G)
            sp.dma_start(out[(NC - 1) * G:NC * G].rearrange("g p d -> p g d"), y_sb[1][:]).then_inc(y_out[1], 16)
            sp.wait_ge(y_out[0], Y_START + 16 * (NC // 2))
            sp.wait_ge(y_out[1], Y_START + 16 * (NC // 2))

        @block.gpsimd
        def _(pool):
            pool.sem_inc(c_att, C_START)
            pool.sem_inc(c_x, C_START)
            pool.memset(ident[:], 0.0).then_inc(s_ident, 1)
            pool.memset(neg_half[:], -0.5).then_inc(s_ident, 1)
            pool.memset(eps_l0[:], 1e-5).then_inc(s_ident, 1)
            pool.memset(eps_l1[:], 1e-6).then_inc(s_ident, 1)
            pool.memset(zero_g[:], 0.0).then_inc(s_ident, 1)
            pool.wait_ge(s_ident, 5)
            pool.affine_select(out=ident[:], in_=ident[:], compare_op=ALU.not_equal, fill=1.0, base=0,
                               pattern=[[-1, P]], channel_multiplier=1).then_inc(s_ident, 1)

            for r in range(2):
                pool.memset(v_sb[r][:], 1.0).then_inc(s_clear, 1)
                pool.memset(kd_sb[r][:], 0.0).then_inc(s_clear, 1)

            def add_bias(i, first, bias, signal):
                for g in range(G):
                    pool.wait_ge(ln_xn, (i + first) * G + G)
                    pool.tensor_tensor(xs(i, g), xs(i, g), bias[:], ALU.add).then_inc(signal, 1)

            def setup_gains():
                pool.wait_ge(w_in[2], 32)
                pool.wait_ge(w_in[1], 32)
                for name, gain_at in FF_L1:
                    if gain_at is not None:
                        w = stage[name]
                        pool.tensor_tensor(scaled[name][:], w[:],
                                           cols[:, gain_at:gain_at + KT].unsqueeze(2).to_broadcast([P, KT, w.shape[2]]),
                                           ALU.mult).then_inc(setup_pool, 1)

            def setup_lo():
                pool.wait_ge(setup_pool, 3)
                for n, (name, gain_at) in enumerate(FF_L1):
                    hi, lo = whl[name]
                    pool.wait_ge(setup_act, n + 1)
                    pool.tensor_tensor(lo[:], (stage if gain_at is None else scaled)[name][:],
                                       hi[:].bitcast(F32), ALU.subtract).then_inc(setup_pool, 1)

            def rstd_of(c, eps):
                pool.wait_ge(ln_mv, c * G + G)
                pool.tensor_tensor(ve[:], mv[:, :, 1], eps[:], ALU.add).then_inc(ln_ve, 1)
                pool.wait_ge(ln_ve, c + 1)
                pool.tensor_tensor(rstd[:], ve[:], neg_half[:], ALU.pow).then_inc(ln_rs, 1)

            def neg_mean_of(c):
                pool.wait_ge(ln_rs, c + 1)
                pool.tensor_tensor(ve[:], mv[:, :, 0], rstd[:], ALU.mult).then_inc(ln_mr, 1)
                pool.wait_ge(ln_mr, c - CC)
                pool.tensor_tensor(neg_mr[:], zero_g[:], ve[:], ALU.subtract).then_inc(ln_nm, 1)
                pool.wait_ge(ln_nm, c - CC)

            rstd_of(0, EPS[CA])
            pool.wait_ge(w_in[3], 16 * len(small_cols))
            setup_gains()
            for first in (CA, CB, CC, CD):
                def norms(i, half, par, first=first):
                    final = isinstance(i, int) and i == NC - 1
                    if first == CC and not (isinstance(i, int) and i < 2):
                        residual(i - 2)
                    if first == CB:
                        add_bias(i, CB, bf2_bc, b_xb)
                    if first == CD:
                        add_bias(i, CD, c2_bc, d_xb)
                    if first == CA and not (isinstance(i, int) and i == 0):
                        add_bias(i, CA, bo_bc, a_xb)
                    if not (final and first == CD):
                        if first >= CC:
                            pool.wait_ge(ln_xn, (i + first + 1) * G)
                        rstd_of(i + first + 1, EPS[first + NC] if final else EPS[first])
                        if first >= CC:
                            neg_mean_of(i + first + 1)
                    if first == CA and isinstance(i, int) and i == 0:
                        setup_lo()
                        pool.wait_ge(setup_dve, setup_at["all"])
                        add_bias(0, CA, bo_bc, a_xb)
                    if first == CC:
                        rows_lo(i, par)
                        add_bias(i, CC, c1_bc, c_xb)

                def rows_lo(e, par):
                    pool.wait_ge(c_rp, e + 1)
                    pool.tensor_tensor(rp[par][32:40, :], rb[32:40, :], rp[par][32:40, :].bitcast(F32), ALU.subtract).then_inc(c_lo, 1)
                    pool.wait_ge(c_lo, e + 1)

                def residual(i):
                    for g in range(G):
                        pool.wait_ge(c_rec, i + 1)
                        wait_for(pool, c_x, i * G + C_START)
                        pool.tensor_tensor(atc[:, g, :].rearrange("p (h d) -> p h d", d=HD),
                                           o_sb[:, g, :].rearrange("p (h c) -> p h c", c=HA)[:, :, 0:HD],
                                           crec[:, g, :].unsqueeze(2).to_broadcast([P, H, HD]), ALU.mult).then_inc(c_att, 1)
                    for g in range(G):
                        pool.wait_ge(c_xb, i * G + g + 1)
                        pool.wait_ge(c_att, i * G + g + 1 + C_START)
                        pool.tensor_tensor(xs(i, g), atc[:, g, :], xs(i, g), ALU.add).then_inc(c_x, 1)
                chunks(pool, norms)
                if first == CC:
                    residual(NC - 2)
                    residual(NC - 1)

        @block.scalar
        def _(act):
            for vec, at in small_cols:
                n = vec.shape[0] // P
                with nc.allow_non_contiguous_dma("a vector as columns"):
                    act.dma_start(cols[:, at:at + n], vec.rearrange("(k p) -> p k", p=P)).then_inc(w_in[3], 16)
            for n, a in enumerate((as1, ad1, as2, ad2)):
                act.dma_start(a_bc[n][:], a.rearrange("h k -> (h k)").partition_broadcast(P)).then_inc(w_in[4], 16)
            for dst, r in ((bo_bc, bo), (bf2_bc, bf2)):
                act.dma_start(dst[:], r.partition_broadcast(P)).then_inc(w_in[4], 16)

            def setup_hi():
                act.wait_ge(setup_pool, 3)
                act.wait_ge(w_in[1], 32)
                for name, gain_at in FF_L1:
                    act.activation(whl[name][0][:], (stage if gain_at is None else scaled)[name][:], ACT.Copy).then_inc(setup_act, 1)

            def ln_hi(c):
                for kt in range(KT):
                    act.wait_ge(ln_t, c * KT + kt + 1)
                    act.activation(xh[:, kt, :], F[kt][:], ACT.Copy).then_inc(ln_xh, 1)

            def a_adj(i, par):
                act.wait_ge(adj_t, i + 1)
                act.activation(ft_sb[par][:].rearrange("p g n -> p (g n)"), F[0][:], ACT.Exp,
                               bias=exp_bias[:, 0:1], scale=2.0).then_inc(a_et, 1)

            def a_qk_out(i, par, n):
                dst = (q_sb, k_sb)[n // 2][par][:, n % 2, :]
                act.wait_ge(a_qk, i * 4 + n + 1)
                act.activation(dst, F[(n + 1) % 2][:], ACT.Identity, bias=bcol[:, n:n + 1]).then_inc(a_qkev, 1)

            def a_v_out(i, par, n):
                act.wait_ge(a_v, i * 2 + n + 1)
                for e in range(2):
                    r = act.activation(v_sb[par][:, (2 * n + e) * H * HA:(2 * n + e + 1) * H * HA].rearrange("p (h c) -> p h c", c=HA)[:, :, 0:HD],
                                       F[1 - n][:, e * D:(e + 1) * D].rearrange("p (h c) -> p h c", c=HD), ACT.Copy)
                r.then_inc(a_vev, 1)

            def a_front(i, par, g):
                if g == 0:
                    a_qk_out(i, par, 0)
                if g == 1:
                    a_qk_out(i, par, 2)
                if g == 3:
                    a_v_out(i, par, 0)
                    a_v_out(i, par, 1)

            def a_front_early(i, par, g):
                if g == 0:
                    ln_hi(i + CA)
                    a_adj(i, par)
                    if isinstance(i, int) and i == 0:
                        act.wait_ge(setup_dve, setup_at["projections"])
                if g == 1:
                    a_qk_out(i, par, 1)
                if g == 2:
                    a_qk_out(i, par, 3)

            def a_exps(s):
                act.wait_ge(a_nm, s + 1)
                wait_for(act, a_tt, s)
                for h in range(H):
                    r = act.activation(e_sb[:, h, :], L_ps[:, h, :], ACT.Exp, bias=nmx[:, h:h + 1], scale=LOGIT_SCALE)
                r.then_inc(a_e, 1)

            def a_ah_out(s):
                act.wait_ge(a_at, s + 1)
                act.activation(ah[:], WO_ps, ACT.Copy).then_inc(a_ah, 1)

            def a_step(i, half, par):
                for g in range(G):
                    s = i * G + (g - G)
                    first = isinstance(i, int) and i == 0
                    if g == 0:
                        a_front_early(i, par, g)
                    if not first:
                        a_exps(s)
                    if g > 0:
                        a_front_early(i, par, g)
                    if not (first or (isinstance(s, int) and s == 0)):
                        a_ah_out(s - 1)
                    a_front(i, par, g)
                if isinstance(i, int) and i == 0:
                    setup_hi()
            act.wait_ge(s_ident, 6)
            act.activation(warm[:], zero_g[:], ACT.Exp)
            act.wait_ge(setup_dve, setup_at["constants"])
            act.wait_ge(s_clear, 4)
            chunks(act, a_step)
            ln_hi(CB)
            for g in range(G):
                s = (NC - 1) * G + g
                a_exps(s)
                a_ah_out(s - 1)
            a_ah_out(NG - 1)

            def b_step(i, half, par):
                for f in range(FT):
                    act.wait_ge(b_h, i * FT + f + 1)
                    if f == 0:
                        wait_for(act, b_o, i * G)
                    wait_for(act, b_gl, i * FT + (f - 1))
                    act.activation(gf[f % 2][:], BK[:, f % 4, :], ACT.Gelu, bias=bcol[:, 6 + f:7 + f])
                    act.activation(gh[:, f, :], BK[:, f % 4, :], ACT.Gelu, bias=bcol[:, 6 + f:7 + f]).then_inc(b_gh, 1)
                ln_hi(i + CB + 1)
            act.activation(warm[:], zero_g[:], ACT.Gelu)
            act.wait_ge(a_x, NG)
            chunks(act, b_step)
            act.activation(warm[:], zero_g[:], ACT.Exp)

            def normalise(i, first, graphs):
                if isinstance(i, int) and i == NC - 1:
                    if first == CD:
                        return
                    nxt = 0
                else:
                    nxt = i + 1
                c = i + first + 1
                act.wait_ge(ln_nm, c - CC)
                act.wait_ge(ln_t, c * KT)
                for g in graphs:
                    act.activation(xn[:, g, :], xs(nxt, g), ACT.Identity, scale=rstd[:, g:g + 1],
                                   bias=neg_mr[:, g:g + 1]).then_inc(ln_xn, 1)

            def c_front(i, par, first):
                c = i + first
                if not (isinstance(c, int) and c == CC):
                    ln_hi(c)
                if first == CD and not (isinstance(i, int) and i == 0):
                    d_hb(i - 1, 1 - par, 1)
                act.wait_ge(adj_t, c - NC + 1)
                act.activation(gt_sb[par][:].rearrange("p g n -> p (g n)"), F[0][:], ACT.Exp).then_inc(c_gt, 1)
                if first == CC:
                    act.wait_ge(c_rows, i * 5 + 5)
                    wait_for(act, c_lo, i)
                    act.activation(rb[0:ROWS, :], u_sb[:], ACT.Exp).then_inc(c_rb, 1)
                    act.activation(rp[par][:], u_sb[:], ACT.Exp).then_inc(c_rp, 1)
                    normalise(i, CC, range(G))
                else:
                    act.wait_ge(c_rows, (i + NC) * 5 + 5)
                    if isinstance(i, int) and i == 0:
                        act.wait_ge(c_lo, NC)
                    else:
                        act.wait_ge(d_bc, i)
                    act.activation(rb[0:ROWS, :], u_sb[:], ACT.Exp).then_inc(c_rb, 1)
                    normalise(i, CD, (0, 1, 2))

            def d_hb(i, par, n):
                e = i + NC
                act.wait_ge(c_bq, e + 1)
                act.wait_ge(c_h, e * 2 + 1 + n)
                for g in range(2 * n, 2 * n + 2):
                    r = act.activation(hb[par][:, g * (D + 1):g * (D + 1) + D],
                                       BK[:, 1 + n, (g % 2) * D:(g % 2 + 1) * D],
                                       ACT.Copy, scale=bq_sb[par][:, g, 8:9])
                r.then_inc(c_hb, 1)

            act.wait_ge(c_zero, 4)

            def c_out_copy(i):
                wait_for(act, c_att, i * G + C_START)
                for g in range(G):
                    act.wait_ge(c_o, (i + 1) * H)
                    act.activation(o_sb[:, g, :], BK[:, 2 + g, 0:H * HA], ACT.Copy).then_inc(c_ev, 1)

            def c1_step(i, half, par):
                if not (isinstance(i, int) and i < 2):
                    c_out_copy(i - 2)
                c_front(i, par, CC)
            chunks(act, c1_step)
            c_out_copy(NC - 2)
            c_out_copy(NC - 1)

            def c2_step(i, half, par):
                c_front(i, par, CD)
                d_hb(i, par, 0)
            chunks(act, c2_step)
            d_hb(NC - 1, 1, 1)

        @block.tensor
        def _(pe):
            def three(dst, w_hi, w_lo, m_hi, m_lo, start, stop):
                pe.matmul(dst, w_hi, m_hi, start=start, stop=False)
                pe.matmul(dst, w_hi, m_lo, start=False, stop=False)
                return pe.matmul(dst, w_lo, m_hi, start=False, stop=stop)

            def wide(dst, name, at):
                hi, lo = whl[name]
                for kt in range(KT):
                    r = three(dst, hi[:, kt, at:at + P], lo[:, kt, at:at + P], xh[:, kt, :], xl[:, kt, :], kt == 0, kt == KT - 1)
                return r

            def tall(dst, name, g, start):
                hi, lo = whl[name]
                for kt in range(KT):
                    n = slice(g * P, (g + 1) * P)
                    pe.matmul(dst, xh[:, kt, n], hi[:, kt, :], start=start and kt == 0, stop=False, skip_group_check=True)
                    pe.matmul(dst, xl[:, kt, n], hi[:, kt, :], start=False, stop=False, skip_group_check=True)
                    r = pe.matmul(dst, xh[:, kt, n], lo[:, kt, :], start=False, stop=(kt == KT - 1), skip_group_check=True)
                return r

            def ln_turn(c):
                pe.wait_ge(ln_xn, c * G + G)
                for kt in range(KT):
                    for g in range(G):
                        r = pe.transpose(F[kt][:, g * P:(g + 1) * P], xn[:, g, kt * P:(kt + 1) * P], ident[:])
                    r.then_inc(ln_t, 1)

            def bias_column(w, m, width, b_at, rows, col):
                for kt in range(KT):
                    r = pe.matmul(BK[0:rows, 4, col:col + 1], w[:, kt, m:m + width], cols[:, b_at + kt:b_at + kt + 1],
                                  start=(kt == 0), stop=(kt == KT - 1), skip_group_check=True)
                return r

            pe.wait_ge(w_in[3], 16 * len(small_cols))
            pe.wait_ge(w_in[0], 64)
            for n, name in enumerate(("wq", "wk", "wv")):
                for m in range(KT):
                    r = bias_column(stage[name], m * P, P, 0, P, 2 * n + m)
            r.then_inc(setup_pe, 1)

            def setup_biases():
                pe.wait_ge(w_in[1], 32)
                pe.wait_ge(w_in[2], 32)
                for m in range(FT):
                    bias_column(stage["wf1"], m * P, P, 12, P, 6 + m)
                pe.wait_ge(setup_dve, setup_at["rows"])
                for layer, b_at in ((0, 22), (1, 26)):
                    bias_column(wc[:, layer], 0, ROWS, b_at, ROWS, 14 + layer)
                for n, (dst, name) in enumerate(((BK[:, 3, 0:D], "wo"), (BK[:, 5, 0:D], "w1"), (BK[:, 5, D:2 * D], "w2"))):
                    for kt in range(KT):
                        r = pe.matmul(dst, b_wide[n][:, kt, :], stage[name][:, kt, :],
                                      start=(kt == 0), stop=(kt == KT - 1), skip_group_check=True)
                r.then_inc(setup_pe, 1)

            pe.wait_ge(s_ident, 6)

            def a_proj(i, n):
                wait_for(pe, *(((ln_xl, (i + CA) * KT + 2)), (a_ft, i + 1), (a_qkev, i * 4 + 1), (a_qkev, i * 4 + 2))[n])
                wide(F[(n + 1) % 2][:], ("wq", "wk")[n // 2], (n % 2) * P).then_inc(a_qk, 1)

            def a_vproj(i, g):
                n, e = g // 2, g % 2
                pe.wait_ge(a_qkev, i * 4 + 3 + n)
                r = tall(F[1 - n][:, e * D:(e + 1) * D], "wv", g, e == 0)
                if e == 1:
                    r.then_inc(a_v, 1)

            def adj_turn(c, half, par, first):
                before = {CA: 0, CC: NC // 2, CD: NC}[first]
                pe.wait_ge(adj_ld[par], (half + 1 + before) * 16)
                pe.wait_ge(ln_xl, c * KT + 1)
                for g in range(G):
                    r = pe.transpose(F[0][:, g * P:(g + 1) * P], adj_in[par][:, g, :], ident[:])
                r.then_inc(adj_t, 1)

            def a_front_a(i, g):
                for n in ((0,), (1,), (3,), ())[g]:
                    a_proj(i, n)
                if g == 3:
                    a_vproj(i, 1)
                    a_vproj(i, 2)

            def a_front_b(i, g):
                if g == 1:
                    a_proj(i, 2)
                if g == 2:
                    a_vproj(i, 0)
                if g == 3:
                    a_vproj(i, 3)

            def a_logits(s, i, par, g):
                pe.wait_ge(a_qkev, i * 4 + 4)
                wait_for(pe, a_e, s)
                pe.wait_ge(kd_ld[g % 2], (i * 2 + (g // 2 + 1)) * 64)
                for t in range(2):
                    r = pe.matmul(BK[:, t, :], q_sb[par][:, t, g * P:(g + 1) * P], kd_sb[g % 2][:, t].rearrange("p h n -> p (h n)"),
                                  start=True, stop=True)
                r.then_inc(a_l, 1)

            def a_turn(s):
                pe.wait_ge(a_e, s + 1)
                wait_for(pe, a_pt, s)
                for h in range(H):
                    r = pe.transpose(ET_ps[:, h, :], e_sb[:, h, :], ident[:])
                r.then_inc(a_tt, 1)

            def a_av(s, i, par, g):
                pe.wait_ge(a_vev, i * 2 + 2)
                pe.wait_ge(a_pt, s + 1)
                wait_for(pe, a_att, s)
                for h in range(H):
                    r = pe.matmul(head_out(4, h), pt_sb[:, h, :], head_in(v_sb[par], g, h), start=True, stop=True)
                r.then_inc(a_o, 1)

            def a_attn_turn(s):
                pe.wait_ge(a_att, s + 1)
                wait_for(pe, a_x, s)
                for kt in range(KT):
                    r = pe.transpose(BK[:, 5, kt * P:(kt + 1) * P], att[:, kt * P:(kt + 1) * P], ident[:])
                r.then_inc(a_at, 1)

            def a_out(s):
                pe.wait_ge(a_al, s + 1)
                hi, lo = whl["wo"]
                for kt in range(KT):
                    n = slice(kt * P, (kt + 1) * P)
                    pe.matmul(WO_ps, ah[:, n], hi[:, kt, :], start=(kt == 0), stop=False)
                    pe.matmul(WO_ps, al[:, n], hi[:, kt, :], start=False, stop=False)
                    r = pe.matmul(WO_ps, ah[:, n], lo[:, kt, :], start=False, stop=(kt == KT - 1))
                r.then_inc(a_wo, 1)

            def a_step(i, half, par):
                first = isinstance(i, int) and i == 0
                for g in range(G):
                    s = i * G + (g - G)
                    prev = not (first or (isinstance(s, int) and s == 0))
                    if g == 0:
                        wait_for(pe, a_vev, i * 2)
                        ln_turn(i + CA)
                    if not first:
                        a_logits(s, i - 1, 1 - par, g)
                    if not (first or isinstance(s, int) and s < 2):
                        a_out(s - 2)
                    if g == 0:
                        adj_turn(i + CA, half, par, CA)
                    if g == 0 and first:
                        pe.wait_ge(setup_dve, setup_at["projections"])
                    if prev:
                        a_av(s - 1, *((i - 2, par, G - 1) if g == 0 else (i - 1, 1 - par, g - 1)))
                    a_front_a(i, g)
                    if prev:
                        a_attn_turn(s - 1)
                    a_front_b(i, g)
                    if isinstance(i, int) and i == 1 and g == 0:
                        pe.wait_ge(setup_dve, setup_at["all"])
                    if not first:
                        a_turn(s)
                if first:
                    setup_biases()
            chunks(pe, a_step)
            pe.wait_ge(a_vev, 2 * NC)
            ln_turn(CB)
            for g in range(G):
                s = (NC - 1) * G + g
                a_logits(s, NC - 1, (NC - 1) % 2, g)
                a_out(s - 2)
                a_av(s - 1, (s - 1) // G, (s - 1) // G % 2, (s - 1) % G)
                a_attn_turn(s - 1)
                a_turn(s)
            a_out(NG - 2)
            a_av(NG - 1, NC - 1, (NC - 1) % 2, G - 1)
            a_attn_turn(NG - 1)
            a_out(NG - 1)

            def b_step(i, half, par):
                pe.wait_ge(ln_xl, (i + CB) * KT + 2)
                for f in range(FT):
                    wait_for(pe, b_gh, i * FT + (f - 3))
                    wide(BK[:, f % 4, :], "wf1", f * P).then_inc(b_h, 1)
                ln_turn(i + CB + 1)
                hi, lo = whl["wf2"]
                for g in range(G):
                    dst = BK[:, 4 + g % 2, 0:D]
                    n = slice(g * P, (g + 1) * P)
                    wait_for(pe, b_x, i * G + (g - 1))
                    for f in range(FT):
                        pe.wait_ge(b_gl, i * FT + f + 1)
                        pe.matmul(dst, gh[:, f, n], hi[:, f, :], start=(f == 0), stop=False)
                        pe.matmul(dst, gl[:, f, n], hi[:, f, :], start=False, stop=False)
                        r = pe.matmul(dst, gh[:, f, n], lo[:, f, :], start=False, stop=(f == FT - 1))
                    r.then_inc(b_o, 1)
            pe.wait_ge(a_x, NG)
            pe.wait_ge(setup_act, setup_act_steps)
            pe.wait_ge(setup_pool, setup_pool_steps)
            chunks(pe, b_step)

            def c_turn(i, first):
                c, e = i + first, i + (first - CC)
                if isinstance(c, int) and c == CC:
                    return
                if first == CC or isinstance(i, int) and i == 0:
                    wait_for(pe, c_hb, e * 2)
                else:
                    pe.wait_ge(c_bq, e)
                ln_turn(c)

            def c_st(i, first, kt):
                pe.wait_ge(ln_xl, (i + first) * KT + 2)
                hi, lo = whl[("wst1", "wst2")[(first - CC) // NC]]
                r = three(F[1][:], hi[:, kt, :], lo[:, kt, :], xh[:, kt, :], xl[:, kt, :], kt == 0, kt == KT - 1)
                if kt == KT - 1:
                    r.then_inc(c_st_done, 1)

            def c_b_turn(i, first):
                pe.wait_ge(c_rb, i + (first - CC) + 1)
                for g in range(G):
                    r = pe.transpose(F[1][:, g * P:(g + 1) * P], rb[:, g * P:(g + 1) * P], ident[:])
                r.then_inc(c_bqt, 1)

            def c1_front(i, half, par, h):
                if h == 0:
                    c_turn(i, CC)
                if h == 1:
                    adj_turn(i + CC, half, par, CC)
                    c_st(i, CC, 0)
                if h == 2:
                    c_st(i, CC, 1)
                if h == 3:
                    pe.wait_ge(c_gt, i + 1)
                if h == 5:
                    c_b_turn(i, CC)
                if h == 6:
                    pe.wait_ge(c_bq, i + 1)
                for g in {3: (0,), 4: (1,), 6: (2, 3)}.get(h, ()):
                    r = tall(F[g // 2][:, (g % 2) * D:(g % 2 + 1) * D], "w1", g, g % 2 == 0)
                    if g % 2 == 1:
                        r.then_inc(c_h, 1)

            def c_bcast(i, par, h):
                pe.wait_ge(c_rp, i + 1)
                pe.wait_ge(c_lo, i + 1)
                wait_for(pe, c_pp, i * H + (h - 1))
                pe.matmul(BK[:, h % 2, :], sel[:, h, :], rp[par][:], start=True, stop=True).then_inc(c_bc, 1)

            def c_av(i, par, h):
                pe.wait_ge(c_pp, i * H + h + 1)
                if h == 0:
                    pe.wait_ge(c_hb, i * 2 + 2)
                    pe.wait_ge(c_one, i + 1)
                for g in range(G):
                    if h == 0:
                        wait_for(pe, c_ev, i * G + (g - G + 1))
                    r = pe.matmul(head_out(2 + g, h), pp[h % 2][:, g, :], head_in(hb[par], g, h), start=True, stop=True)
                r.then_inc(c_o, 1)

            def c1_step(i, half, par):
                back = not (isinstance(i, int) and i == 0)
                for h in range(H):
                    if back and h < H - 1:
                        c_bcast(i - 1, 1 - par, h + 1)
                    c1_front(i, half, par, h)
                    if h == H - 2:
                        c_bcast(i, par, 0)
                    if back:
                        c_av(i - 1, 1 - par, h)
            pe.wait_ge(b_x, NG)
            chunks(pe, c1_step)
            last = (NC - 1) % 2
            for h in range(H):
                if h < H - 1:
                    c_bcast(NC - 1, last, h + 1)
                c_av(NC - 1, last, h)

            def d_bcast(i):
                pe.wait_ge(c_rb, i + NC + 1)
                wait_for(pe, d_pp, i * G)
                pe.matmul(BK[:, 0, :], sel[0:32, 0, :].bitcast(F32), rb[0:32, :], start=True, stop=True).then_inc(d_bc, 1)

            def d_av(i, par, g):
                if g == 0:
                    pe.wait_ge(c_hb, (i + NC) * 2 + 2)
                    pe.wait_ge(c_one, i + NC + 1)
                pe.wait_ge(d_pp, i * G + g + 1)
                if g == 3:
                    pe.wait_ge(d_y, i * G + 1)
                else:
                    wait_for(pe, d_y, i * G + (g - G + 1 if g else 0))
                pe.matmul(BK[:, D_O[g], 0:D + 1], pp[0][:, g, :], hb[par][:, g * (D + 1):(g + 1) * (D + 1)],
                          start=True, stop=True).then_inc(d_o, 1)

            def d_h(i, g):
                r = tall(BK[:, 1 + g // 2, (g % 2) * D:(g % 2 + 1) * D], "w2", g, g % 2 == 0)
                if g % 2 == 1:
                    r.then_inc(c_h, 1)

            def c2_step(i, half, par):
                back = not (isinstance(i, int) and i == 0)
                c_turn(i, CD)
                if back:
                    d_bcast(i - 1)
                adj_turn(i + CD, half, par, CD)
                for kt in range(KT):
                    c_st(i, CD, kt)
                if back:
                    for g in range(3):
                        d_av(i - 1, 1 - par, g)
                wait_for(pe, c_hb, (i + NC) * 2)
                for g in range(3):
                    d_h(i, g)
                c_b_turn(i, CD)
                d_h(i, 3)
                if back:
                    d_av(i - 1, 1 - par, 3)
            pe.wait_ge(c_ev, NG)
            chunks(pe, c2_step)
            d_bcast(NC - 1)
            for g in range(G):
                d_av(NC - 1, last, g)




_INS = ['x', 'adj', 'L0_gnn_Wq', 'L0_gnn_bq', 'L0_gnn_Wk', 'L0_gnn_bk', 'L0_gnn_Wv', 'L0_gnn_bv', 'L0_gnn_Wo', 'L0_gnn_bo',
        'L0_gnn_g1', 'L0_gnn_b1', 'L0_gnn_g2', 'L0_gnn_b2', 'L0_gnn_Wf1', 'L0_gnn_bf1', 'L0_gnn_Wf2', 'L0_gnn_bf2',
        'L1_gnn_W1', 'L1_gnn_a_src1', 'L1_gnn_a_dst1', 'L1_gnn_g1', 'L1_gnn_b1',
        'L1_gnn_W2', 'L1_gnn_a_src2', 'L1_gnn_a_dst2', 'L1_gnn_g2', 'L1_gnn_b2']


def kernel(**inputs):
    import numpy as _np
    import concourse.bacc as _bacc
    from concourse import mybir as _mybir
    from concourse.bass_utils import run_bass_kernel_spmd as _run

    nc = _bacc.Bacc("TRN2", target_bir_lowering=False, num_devices=1)
    arrays, args = {}, []
    for name in _INS:
        a = _np.ascontiguousarray(inputs[name])
        arrays[f"in_{name}_dram"] = a
        args.append(nc.dram_tensor(f"in_{name}_dram", a.shape, _mybir.dt.from_np(a.dtype), kind="ExternalInput").ap())
    args.append(nc.dram_tensor("out_0_dram", inputs["x"].shape, _mybir.dt.float32, kind="ExternalOutput").ap())
    build(nc, *args)
    r = _run(nc, [arrays], core_ids=[0])
    return r.results[0]["out_0_dram"]
```
